# Optimizing a Trainium2 kernel written in Bass

```python
import numpy as np
import jax
import jax.numpy as jnp

def _softmax(x, axis=-1):
    return jax.nn.softmax(x, axis=axis)

def _gelu(x):
    return jax.nn.gelu(x, approximate=True)

def _silu(x):
    return jax.nn.silu(x)

def _sigmoid(x):
    return jax.nn.sigmoid(x)

def _layernorm(x, axis=-1, eps=1e-05):
    m = jnp.mean(x, axis=axis, keepdims=True)
    v = jnp.var(x, axis=axis, keepdims=True)
    return (x - m) / jnp.sqrt(v + eps)

def _scatter_add(tgt, idx, src, axis=0):
    return tgt.at[idx].add(src)

def _segment_sum(src, seg, n):
    return jax.ops.segment_sum(src, seg, n)
kernel_name = 'mk_gnn_ffn_d2_gnn_r8_ad5448'

def setup_inputs(seed: int=0):
    np.random.seed(seed)
    _w = jnp.asarray

    def _rec_inputs():
        import jax
        import jax.numpy as jnp
        _gk = jax.random.key(seed)
        x = -8.776e-05 + 1 * jax.random.normal(jax.random.fold_in(_gk, 1), (1250, 512), jnp.float32)
        _s = jax.random.randint(jax.random.fold_in(_gk, 2), (20000,), 0, 1250, jnp.int32)
        _d = jax.random.randint(jax.random.fold_in(_gk, 3), (20000,), 0, 1250, jnp.int32)
        _loop = jnp.arange(1250, dtype=jnp.int32)
        src = jnp.concatenate([_s, _d, _loop])
        dst = jnp.concatenate([_d, _s, _loop])
        _o = jnp.argsort(dst, stable=True)
        src = src[_o]
        dst = dst[_o]
        edge_weight = -0.00121341 + 0.998923 * jax.random.normal(jax.random.fold_in(_gk, 13), (41250,), jnp.float32)
        return (x, src, dst, edge_weight)
    x, src, dst, edge_weight = _rec_inputs()

    def _L0_gnn_setup():
        import jax, jax.numpy as jnp
        import numpy as np
        N, D, E = (1250, 512, 20000)

        def _mpconv(x, src, dst, norm, W, b, Wr, br):
            h_in = x
            h = x @ W.T
            msg = norm[:, None] * h[src]
            out = jax.ops.segment_sum(msg, dst, num_segments=N)
            out = out + b
            g = jax.nn.sigmoid(h_in @ Wr.T + br)
            return (1.0 - g) * h_in + g * out
        key = jax.random.key(seed)
        ks = jax.random.split(key, 12)
        s = 1.0 / np.sqrt(D)
        inp = {'x': jax.random.normal(ks[0], (N, D), dtype=jnp.float32), 'edge_index': jax.random.randint(ks[1], (2, E), 0, N, dtype=jnp.int64), 'W1': jax.random.uniform(ks[2], (D, D), jnp.float32, -s, s), 'b1': jnp.zeros((D,), jnp.float32), 'Wr1': jax.random.uniform(ks[3], (D, D), jnp.float32, -s, s), 'br1': jax.random.uniform(ks[4], (D,), jnp.float32, -s, s), 'W2': jax.random.uniform(ks[5], (D, D), jnp.float32, -s, s), 'b2': jnp.zeros((D,), jnp.float32), 'Wr2': jax.random.uniform(ks[6], (D, D), jnp.float32, -s, s), 'br2': jax.random.uniform(ks[7], (D,), jnp.float32, -s, s)}
        return inp
    _L0_gnn_all = _L0_gnn_setup()
    _L0_gnn_in = {k: v for k, v in _L0_gnn_all.items() if k in ('W1', 'b1', 'Wr1', 'br1', 'W2', 'b2', 'Wr2', 'br2')}
    del _L0_gnn_all

    def _L0_ffn_setup():
        import math
        import jax, jax.numpy as jnp
        import numpy as np
        B, T, D, FF, E = (32, 1024, 512, 256, 8)
        CAPACITY_FACTOR = 1.25
        CAP = int(math.ceil(CAPACITY_FACTOR * B * T / E))

        def _bank_residual(x2, Wr, br, W1, b1, W2, b2):
            N, d = x2.shape
            e = Wr.shape[1]
            logits = x2 @ Wr + br
            probs = jax.nn.softmax(logits, axis=-1)
            expert = jnp.argmax(probs, axis=-1)
            gate = jnp.take_along_axis(probs, expert[:, None], axis=-1)[:, 0]
            oneh = jax.nn.one_hot(expert, e, dtype=x2.dtype)
            pos = (jnp.cumsum(oneh, axis=0) * oneh).sum(-1).astype(jnp.int32) - 1
            keep = pos < CAP
            slot = expert.astype(jnp.int32) * CAP + jnp.minimum(pos, CAP - 1)
            xd = jnp.where(keep[:, None], x2, 0.0)
            buf = jnp.zeros((e * CAP, d), x2.dtype).at[slot].add(xd)
            buf = buf.reshape(e, CAP, d)
            h = jax.nn.gelu(jnp.einsum('ecd,edf->ecf', buf, W1) + b1[:, None, :], approximate=False)
            out = jnp.einsum('ecf,efd->ecd', h, W2) + b2[:, None, :]
            y = out.reshape(e * CAP, d)[slot]
            return y * (gate * keep.astype(x2.dtype))[:, None]
        key = jax.random.key(seed)
        ks = jax.random.split(key, 18)
        s = 0.02
        inp = {'x': jax.random.normal(ks[0], (B, T, D), dtype=jnp.float32), 'Wr_sp': jax.random.normal(ks[1], (D, E)) * s, 'br_sp': jnp.zeros((E,), jnp.float32), 'Wr_fq': jax.random.normal(ks[2], (D, E)) * s, 'br_fq': jnp.zeros((E,), jnp.float32), 'Ws1': jax.random.normal(ks[3], (D, FF)) * s, 'bs1': jnp.zeros((FF,), jnp.float32), 'Ws2': jax.random.normal(ks[4], (FF, D)) * s, 'bs2': jnp.zeros((D,), jnp.float32), 'W1_sp': jax.random.normal(ks[5], (E, D, FF)) * s, 'b1_sp': jnp.zeros((E, FF), jnp.float32), 'W2_sp': jax.random.normal(ks[6], (E, FF, D)) * s, 'b2_sp': jnp.zeros((E, D), jnp.float32), 'W1_fq': jax.random.normal(ks[7], (E, D, FF)) * s, 'b1_fq': jnp.zeros((E, FF), jnp.float32), 'W2_fq': jax.random.normal(ks[8], (E, FF, D)) * s, 'b2_fq': jnp.zeros((E, D), jnp.float32)}
        return inp
    _L0_ffn_all = _L0_ffn_setup()
    _L0_ffn_in = {k: v for k, v in _L0_ffn_all.items() if k in ('Wr_sp', 'br_sp', 'Wr_fq', 'br_fq', 'Ws1', 'bs1', 'Ws2', 'bs2', 'W1_sp', 'b1_sp', 'W2_sp', 'b2_sp', 'W1_fq', 'b1_fq', 'W2_fq', 'b2_fq')}
    del _L0_ffn_all

    def _L1_gnn_setup():
        import jax, jax.numpy as jnp
        import numpy as np
        N = 2500
        E = 25000
        D = 512
        H = 512

        def _layernorm(x, gamma, beta, eps=1e-05):
            mu = jnp.mean(x, axis=-1, keepdims=True)
            var = jnp.mean((x - mu) ** 2, axis=-1, keepdims=True)
            return (x - mu) * jax.lax.rsqrt(var + eps) * gamma + beta
        key = jax.random.key(seed)
        ks = jax.random.split(key, 12)
        s = 0.02
        return {'source_features': jax.random.normal(ks[0], (N, D), jnp.float32), 'weighting_gate': jax.random.normal(ks[1], (E,), jnp.float32), 'rel_pair_idx': jax.random.randint(ks[2], (E, 2), 0, N, dtype=jnp.int32), 'Wm': jax.random.normal(ks[3], (D, D // 2), jnp.float32) * s, 'bm': jnp.zeros((D // 2,), jnp.float32), 'W1': jax.random.normal(ks[4], (D, D // 4), jnp.float32) * s, 'b1': jnp.zeros((D // 4,), jnp.float32), 'gamma': jnp.ones((D // 4,), jnp.float32), 'beta': jnp.zeros((D // 4,), jnp.float32), 'W2': jax.random.normal(ks[5], (D // 4, H), jnp.float32) * s, 'b2': jnp.zeros((H,), jnp.float32)}
    _L1_gnn_all = _L1_gnn_setup()
    _L1_gnn_in = {k: v for k, v in _L1_gnn_all.items() if k in ('Wm', 'bm', 'W1', 'b1', 'gamma', 'beta', 'W2', 'b2')}
    del _L1_gnn_all

    def _L1_ffn_setup():
        import jax, jax.numpy as jnp
        import numpy as np
        T = 512
        B = 64
        C = 1024

        def _triu_apply(x, W, b):
            Wm = jnp.tril(W)
            return jnp.einsum('bct,st->bcs', x, Wm) + b
        key = jax.random.key(seed)
        ks = jax.random.split(key, 5)
        x = jax.random.normal(ks[0], (B, C, T), dtype=jnp.float32)
        scale = 1.0 / jnp.sqrt(jnp.arange(1, T + 1, dtype=jnp.float32))[:, None]
        W1 = jax.random.uniform(ks[1], (T, T), jnp.float32, -1.0, 1.0) * scale
        b1 = jax.random.uniform(ks[2], (T,), jnp.float32, -1.0, 1.0) * scale[:, 0]
        W2 = jax.random.uniform(ks[3], (T, T), jnp.float32, -1.0, 1.0) * scale
        b2 = jax.random.uniform(ks[4], (T,), jnp.float32, -1.0, 1.0) * scale[:, 0]
        return {'x': x, 'W1': W1, 'b1': b1, 'W2': W2, 'b2': b2}
    _L1_ffn_all = _L1_ffn_setup()
    _L1_ffn_in = {k: v for k, v in _L1_ffn_all.items() if k in ('W1', 'b1', 'W2', 'b2')}
    del _L1_ffn_all
    return {'x': x, 'src': src, 'dst': dst, 'edge_weight': edge_weight, 'L0_gnn_W1': _L0_gnn_in['W1'], 'L0_gnn_b1': _L0_gnn_in['b1'], 'L0_gnn_Wr1': _L0_gnn_in['Wr1'], 'L0_gnn_br1': _L0_gnn_in['br1'], 'L0_gnn_W2': _L0_gnn_in['W2'], 'L0_gnn_b2': _L0_gnn_in['b2'], 'L0_gnn_Wr2': _L0_gnn_in['Wr2'], 'L0_gnn_br2': _L0_gnn_in['br2'], 'L0_ffn_Wr_sp': _L0_ffn_in['Wr_sp'], 'L0_ffn_br_sp': _L0_ffn_in['br_sp'], 'L0_ffn_Wr_fq': _L0_ffn_in['Wr_fq'], 'L0_ffn_br_fq': _L0_ffn_in['br_fq'], 'L0_ffn_Ws1': _L0_ffn_in['Ws1'], 'L0_ffn_bs1': _L0_ffn_in['bs1'], 'L0_ffn_Ws2': _L0_ffn_in['Ws2'], 'L0_ffn_bs2': _L0_ffn_in['bs2'], 'L0_ffn_W1_sp': _L0_ffn_in['W1_sp'], 'L0_ffn_b1_sp': _L0_ffn_in['b1_sp'], 'L0_ffn_W2_sp': _L0_ffn_in['W2_sp'], 'L0_ffn_b2_sp': _L0_ffn_in['b2_sp'], 'L0_ffn_W1_fq': _L0_ffn_in['W1_fq'], 'L0_ffn_b1_fq': _L0_ffn_in['b1_fq'], 'L0_ffn_W2_fq': _L0_ffn_in['W2_fq'], 'L0_ffn_b2_fq': _L0_ffn_in['b2_fq'], 'L1_gnn_Wm': _L1_gnn_in['Wm'], 'L1_gnn_bm': _L1_gnn_in['bm'], 'L1_gnn_W1': _L1_gnn_in['W1'], 'L1_gnn_b1': _L1_gnn_in['b1'], 'L1_gnn_gamma': _L1_gnn_in['gamma'], 'L1_gnn_beta': _L1_gnn_in['beta'], 'L1_gnn_W2': _L1_gnn_in['W2'], 'L1_gnn_b2': _L1_gnn_in['b2'], 'L1_ffn_W1': _L1_ffn_in['W1'], 'L1_ffn_b1': _L1_ffn_in['b1'], 'L1_ffn_W2': _L1_ffn_in['W2'], 'L1_ffn_b2': _L1_ffn_in['b2']}

def reference(x, src, dst, edge_weight, L0_gnn_W1, L0_gnn_b1, L0_gnn_Wr1, L0_gnn_br1, L0_gnn_W2, L0_gnn_b2, L0_gnn_Wr2, L0_gnn_br2, L0_ffn_Wr_sp, L0_ffn_br_sp, L0_ffn_Wr_fq, L0_ffn_br_fq, L0_ffn_Ws1, L0_ffn_bs1, L0_ffn_Ws2, L0_ffn_bs2, L0_ffn_W1_sp, L0_ffn_b1_sp, L0_ffn_W2_sp, L0_ffn_b2_sp, L0_ffn_W1_fq, L0_ffn_b1_fq, L0_ffn_W2_fq, L0_ffn_b2_fq, L1_gnn_Wm, L1_gnn_bm, L1_gnn_W1, L1_gnn_b1, L1_gnn_gamma, L1_gnn_beta, L1_gnn_W2, L1_gnn_b2, L1_ffn_W1, L1_ffn_b1, L1_ffn_W2, L1_ffn_b2):
    import jax
    import jax.numpy as jnp

    def _L0_gnn_ref(x, edge_index, W1, b1, Wr1, br1, W2, b2, Wr2, br2):
        import jax, jax.numpy as jnp
        import numpy as np
        N, D, E = (1250, 512, 20000)

        def _mpconv(x, src, dst, norm, W, b, Wr, br):
            h_in = x
            h = x @ W.T
            msg = norm[:, None] * h[src]
            out = jax.ops.segment_sum(msg, dst, num_segments=N)
            out = out + b
            g = jax.nn.sigmoid(h_in @ Wr.T + br)
            return (1.0 - g) * h_in + g * out
        loops = jnp.arange(N, dtype=edge_index.dtype)
        src = jnp.concatenate([edge_index[0], loops])
        dst = jnp.concatenate([edge_index[1], loops])
        deg = jax.ops.segment_sum(jnp.ones_like(dst, dtype=x.dtype), dst, num_segments=N)
        dis = jnp.where(deg > 0, jax.lax.rsqrt(jnp.maximum(deg, 1e-30)), 0.0)
        norm = dis[src] * dis[dst]
        h = _mpconv(x, src, dst, norm, W1, b1, Wr1, br1)
        h = jax.nn.relu(h)
        h = _mpconv(h, src, dst, norm, W2, b2, Wr2, br2)
        h = jax.nn.relu(h)
        return h

    def _L0_ffn_ref(x, Wr_sp, br_sp, Wr_fq, br_fq, Ws1, bs1, Ws2, bs2, W1_sp, b1_sp, W2_sp, b2_sp, W1_fq, b1_fq, W2_fq, b2_fq):
        import math
        import jax, jax.numpy as jnp
        import numpy as np
        B, T, D, FF, E = (32, 1024, 512, 256, 8)
        CAPACITY_FACTOR = 1.25
        CAP = int(math.ceil(CAPACITY_FACTOR * B * T / E))

        def _bank_residual(x2, Wr, br, W1, b1, W2, b2):
            N, d = x2.shape
            e = Wr.shape[1]
            logits = x2 @ Wr + br
            probs = jax.nn.softmax(logits, axis=-1)
            expert = jnp.argmax(probs, axis=-1)
            gate = jnp.take_along_axis(probs, expert[:, None], axis=-1)[:, 0]
            oneh = jax.nn.one_hot(expert, e, dtype=x2.dtype)
            pos = (jnp.cumsum(oneh, axis=0) * oneh).sum(-1).astype(jnp.int32) - 1
            keep = pos < CAP
            slot = expert.astype(jnp.int32) * CAP + jnp.minimum(pos, CAP - 1)
            xd = jnp.where(keep[:, None], x2, 0.0)
            buf = jnp.zeros((e * CAP, d), x2.dtype).at[slot].add(xd)
            buf = buf.reshape(e, CAP, d)
            h = jax.nn.gelu(jnp.einsum('ecd,edf->ecf', buf, W1) + b1[:, None, :], approximate=False)
            out = jnp.einsum('ecf,efd->ecd', h, W2) + b2[:, None, :]
            y = out.reshape(e * CAP, d)[slot]
            return y * (gate * keep.astype(x2.dtype))[:, None]
        b, t, d = x.shape
        x2 = x.reshape(b * t, d)
        shared = jax.nn.gelu(x2 @ Ws1 + bs1, approximate=False) @ Ws2 + bs2
        y = shared
        y = y + _bank_residual(x2, Wr_sp, br_sp, W1_sp, b1_sp, W2_sp, b2_sp)
        y = y + _bank_residual(x2, Wr_fq, br_fq, W1_fq, b1_fq, W2_fq, b2_fq)
        return y.reshape(b, t, d)

    def _L1_gnn_ref(source_features, weighting_gate, rel_pair_idx, Wm, bm, W1, b1, gamma, beta, W2, b2):
        import jax, jax.numpy as jnp
        import numpy as np
        N = 2500
        E = 25000
        D = 512
        H = 512

        def _layernorm(x, gamma, beta, eps=1e-05):
            mu = jnp.mean(x, axis=-1, keepdims=True)
            var = jnp.mean((x - mu) ** 2, axis=-1, keepdims=True)
            return (x - mu) * jax.lax.rsqrt(var + eps) * gamma + beta
        src = rel_pair_idx[:, 0]
        dst = rel_pair_idx[:, 1]
        n_nodes = source_features.shape[0]
        m = jnp.maximum(jnp.max(weighting_gate), jnp.float32(0.0))
        exp_e = jnp.exp(weighting_gate - m)
        row_sum = jax.ops.segment_sum(exp_e, src, num_segments=n_nodes)
        atten_e = exp_e / (row_sum[src] + 1e-06)
        Mfeat = source_features @ Wm + bm
        out0 = jax.ops.segment_sum(atten_e[:, None] * Mfeat[dst], src, num_segments=n_nodes)
        out1 = jax.ops.segment_sum(atten_e[:, None] * Mfeat[src], dst, num_segments=n_nodes)
        message_feats = jnp.concatenate([out0, out1], axis=-1)
        h = message_feats @ W1 + b1
        h = jax.nn.relu(_layernorm(h, gamma, beta))
        h = jax.nn.relu(h @ W2 + b2)
        valid = (row_sum > 0)[:, None]
        return jnp.where(valid, h, jnp.float32(0.0))

    def _L1_ffn_ref(x, W1, b1, W2, b2):
        import jax, jax.numpy as jnp
        import numpy as np
        T = 512
        B = 64
        C = 1024

        def _triu_apply(x, W, b):
            Wm = jnp.tril(W)
            return jnp.einsum('bct,st->bcs', x, Wm) + b
        h = _triu_apply(x, W1, b1)
        h = jax.nn.gelu(h, approximate=False)
        return _triu_apply(h, W2, b2)
    edge_index = jnp.stack([src, dst])
    edge_index_t = jnp.stack([src, dst], axis=1)
    x = x + _L0_gnn_ref(_layernorm(x, axis=-1), edge_index, L0_gnn_W1, L0_gnn_b1, L0_gnn_Wr1, L0_gnn_br1, L0_gnn_W2, L0_gnn_b2, L0_gnn_Wr2, L0_gnn_br2)
    x = x + _L0_ffn_ref(_layernorm(x, axis=-1)[None], L0_ffn_Wr_sp, L0_ffn_br_sp, L0_ffn_Wr_fq, L0_ffn_br_fq, L0_ffn_Ws1, L0_ffn_bs1, L0_ffn_Ws2, L0_ffn_bs2, L0_ffn_W1_sp, L0_ffn_b1_sp, L0_ffn_W2_sp, L0_ffn_b2_sp, L0_ffn_W1_fq, L0_ffn_b1_fq, L0_ffn_W2_fq, L0_ffn_b2_fq)[0]
    x = x + _L1_gnn_ref(_layernorm(x, axis=-1), edge_weight, edge_index_t, L1_gnn_Wm, L1_gnn_bm, L1_gnn_W1, L1_gnn_b1, L1_gnn_gamma, L1_gnn_beta, L1_gnn_W2, L1_gnn_b2)
    x = x + _L1_ffn_ref(_layernorm(x, axis=-1)[None], L1_ffn_W1, L1_ffn_b1, L1_ffn_W2, L1_ffn_b2)[0]
    return x

_drawn_inputs = setup_inputs


def setup_inputs(seed=0):
    import zlib

    import numpy as np

    out = dict(_drawn_inputs(seed))
    spreads = {'L0_gnn_b1': (0.0, 0.478),
     'L0_gnn_b2': (0.0, 0.1),
     'L0_ffn_br_sp': (0.0, 0.596),
     'L0_ffn_br_fq': (0.0, 0.719),
     'L0_ffn_bs1': (0.0, 0.501),
     'L0_ffn_bs2': (0.0, 0.1),
     'L0_ffn_b1_sp': (0.0, 0.8),
     'L0_ffn_b2_sp': (0.0, 0.396),
     'L0_ffn_b1_fq': (0.0, 0.8),
     'L0_ffn_b2_fq': (0.0, 0.394),
     'L1_gnn_bm': (0.0, 0.1),
     'L1_gnn_b1': (0.0, 0.1),
     'L1_gnn_gamma': (1.0, 0.6),
     'L1_gnn_beta': (0.0, 0.75),
     'L1_gnn_b2': (0.0, 0.1)}
    factors = {'L0_gnn_W1': 3.539,
     'L0_gnn_br1': 8.0,
     'L0_gnn_Wr2': 3.158,
     'L0_gnn_br2': 8.0,
     'L0_ffn_W1_sp': 3.565,
     'L0_ffn_W2_sp': 3.345,
     'L0_ffn_W1_fq': 3.568,
     'L0_ffn_W2_fq': 3.339}
    for name, (base, spread) in spreads.items():
        noise = np.random.default_rng([zlib.crc32(name.encode()), seed]).standard_normal(out[name].shape)
        drawn = base * np.exp(spread * noise) if base else spread * noise
        out[name] = jnp.asarray(drawn.astype(out[name].dtype))
    for name, factor in factors.items():
        out[name] = (out[name] * factor).astype(out[name].dtype)
    return out
```

```python
from contextlib import ExitStack

import concourse.bass as bass
import concourse.mybir as mybir
from concourse.alu_op_type import AluOpType as ALU

F32 = mybir.dt.float32
BF16 = mybir.dt.bfloat16
I32 = mybir.dt.int32
ACT = mybir.ActivationFunctionType
AX = mybir.AxisListType
ds = bass.ds

P = 128
N = 1250
NT = -(-N // P)
NP = NT * P
LAST = N - (NT - 1) * P
D = 512
KD = D // P
CH = 256
NC = NP // CH
TPC = CH // P
E = 41250
SUB = 3
CE = SUB * P
Q = -(-E // CE)
W = 16
KW = NT * W
CW = NP + W
PASSES = -(-NP // W)
FF = 256
NE = 8
ST = (N - NE) // P + NE
SLOTS = ST * P
EPS = 1e-5
FAR = 4096.0

BIAS_COLS = {}
_at = 0
for _name, _n in (("gnn_b1", 4), ("gnn_br1", 4), ("gnn_b2", 4), ("gnn_br2", 4), ("bs1", 2),
                  ("l1_b1", 1), ("ffn_b1", 4)):
    BIAS_COLS[_name] = _at
    _at += _n
NBIAS = _at
BIAS_ROWS = {}
_at = 0
for _name, _n in (("bm", FF), ("gamma", P), ("beta", P), ("l1_b2", D), ("ffn_b2", D)):
    BIAS_ROWS[_name] = (_at, _n)
    _at += _n
NROW = _at


class Chain:

    def __init__(self, eng, sem):
        self.eng, self.sem, self.base, self.n = eng, sem, 0, 0

    def at(self, base):
        self.base, self.n = base, 0

    def mark(self, ins):
        ins.then_inc(self.sem, 1)
        self.n += 1
        return self.base + self.n

    def wait(self, back=0):
        self.eng.wait_ge(self.sem, self.base + self.n - back)


def after(eng, sem, value):
    if not isinstance(value, int) or value > 0:
        eng.wait_ge(sem, value)


def looped(eng, count, body):
    body(0)
    with eng.Fori(1, count) as i:
        body(i)


def build(nc, a, out, routed, expert_out):
    with ExitStack() as top:
        def sb(ctx, name, shape, dt=F32):
            return ctx.enter_context(nc.sbuf_tensor(name, shape, dt))

        def sems(ctx, *names):
            return [ctx.enter_context(nc.semaphore(n)) for n in names]

        cleared_slots, = sems(top, "cleared_slots")
        first_reused = cleared_slots.num + 1

        PS = [top.enter_context(nc.psum_tensor(f"PS{i}", [P, 512], F32)) for i in range(8)]

        X = sb(top, "X", [P, NT, D])
        ident = sb(top, "ident", [P, P])
        ones = sb(top, "ones", [P, P])
        iota = sb(top, "iota", [P, KW, SUB], BF16)
        bcol = sb(top, "bcol", [P, NBIAS])
        eps = sb(top, "eps", [P, 1])
        stats = sb(top, "stats", [P, NT, 6])
        mv = sb(top, "mv", [P, NT, 2])
        std = sb(top, "std", [P, NT])
        rstd = sb(top, "rstd", [P, NT])
        key = sb(top, "key", [P, Q, SUB], BF16)
        srow = sb(top, "srow", [P, Q, SUB], BF16)
        part = sb(top, "part", [P, Q, 3, SUB], BF16)
        first = sb(top, "first", [1, Q])
        base_row = sb(top, "base_row", [1, Q], I32)
        flag = sb(top, "flag", [1, 1], I32)
        rel = sb(top, "rel", [Q, CE])
        sbw = sb(top, "sbw", [Q, CE])

        def tile_of(t3, t):
            return t3[:, ds(t, 1), :].rearrange("p a d -> p (a d)")

        with ExitStack() as ctx:
            s32 = sb(ctx, "s32", [Q, CE], I32)
            d32 = sb(ctx, "d32", [Q, CE], I32)
            wrow = sb(ctx, "wrow", [Q, CE])
            lo32 = sb(ctx, "lo32", [Q, CE], I32)
            hi32 = sb(ctx, "hi32", [Q, CE], I32)
            srowr = sb(ctx, "srowr", [Q, CE])
            past = sb(ctx, "past", [Q, CE])
            keyr = sb(ctx, "keyr", [Q, CE])
            est = sb(ctx, "est", [Q, 4])
            fl = sb(ctx, "fl", [1, 4])
            negmax = sb(ctx, "negmax", [P, 1])
            wexp = sb(ctx, "wexp", [P, Q, SUB])
            edges_in, consts_in, x_in = sems(ctx, "edges_in", "consts_in", "x_in")
            pads, consts, ident_zero = sems(ctx, "pads", "consts", "ident_zero")
            step, spans, keys = sems(ctx, "prep_step", "spans", "keys")
            spans_T, tables_T, tables, wmax, wmax_all, weights = sems(
                ctx, "spans_T", "tables_T", "tables_done", "wmax", "wmax_all", "weights")
            block = ctx.enter_context(nc.Block())

            @block.sync
            def _(sp):
                full, rest = Q - 1, E - (Q - 1) * CE
                sp.wait_ge(pads, 4)
                for t, e in ((s32, a["src"]), (d32, a["dst"]), (wrow, a["edge_weight"])):
                    sp.dma_start(t[0:full, :], e[0:full * CE].rearrange("(q e) -> q e", e=CE)).then_inc(edges_in, 16)
                    sp.dma_start(t[full:Q, 0:rest], e[full * CE:E].rearrange("(q e) -> q e", q=1)).then_inc(edges_in, 16)
                sp.dma_start(X[:, 0:NT - 1, :], a["x"][0:(NT - 1) * P, :].rearrange("(t p) d -> p t d", p=P)).then_inc(x_in, 16)
                sp.dma_start(X[0:LAST, NT - 1, :], a["x"][(NT - 1) * P:N, :]).then_inc(x_in, 16)
                sp.dma_start(bcol[:, :], a["bias_cols"]).then_inc(consts_in, 16)
                sp.wait_ge(x_in, 32)
                sp.wait_ge(consts_in, 16)

            @block.gpsimd
            def _(pool):
                pool.memset(s32[:, :], 4 * NP).then_inc(pads, 1)
                pool.memset(d32[:, :], N - 1).then_inc(pads, 1)
                pool.memset(wrow[:, :], 0.0).then_inc(pads, 1)
                pool.memset(X[:, NT - 1, :], 0.0).then_inc(pads, 1)
                pool.memset(ident[:, :], 0.0).then_inc(ident_zero, 1)
                pool.memset(ones[:, :], 1.0).then_inc(consts, 1)
                pool.memset(eps[:, :], EPS).then_inc(consts, 1)
                pool.iota(iota[:, :, :], pattern=[[1, KW], [0, SUB]], base=0, channel_multiplier=0,
                          allow_small_or_imprecise_dtypes=True).then_inc(consts, 1)
                pool.wait_ge(ident_zero, 1)
                pool.affine_select(out=ident[:, :], in_=ident[:, :], compare_op=ALU.not_equal, fill=1.0, base=0,
                                   pattern=[[-1, P]], channel_multiplier=1).then_inc(consts, 1)

            @block.vector
            def _(dve):
                ch = Chain(dve, step)
                dve.wait_ge(edges_in, 96)
                ch.mark(dve.tensor_scalar(lo32[:, :], s32[:, :], P - 1, None, ALU.bitwise_and))
                ch.mark(dve.tensor_scalar(hi32[:, :], s32[:, :], 7, None, ALU.arith_shift_right))
                ch.mark(dve.tensor_copy(rel[:, :], d32[:, :]))
                ch.wait()
                ch.mark(dve.tensor_scalar(sbw[:, :], hi32[:, :], float(W), None, ALU.mult))
                ch.mark(dve.tensor_reduce(est[:, 0:1], rel[:, :], AX.X, ALU.min))
                ch.mark(dve.tensor_reduce(est[:, 3:4], rel[:, :], AX.X, ALU.max))
                ch.mark(dve.tensor_reduce(est[:, 2:3], wrow[:, :], AX.X, ALU.max))
                ch.wait()
                dve.tensor_tensor(est[:, 1:2], est[:, 3:4], est[:, 0:1], ALU.subtract).then_inc(spans, 1)
                ch.mark(dve.tensor_scalar(rel[:, :], rel[:, :], est[:, 0:1], None, ALU.subtract))
                ch.wait()
                ch.mark(dve.tensor_scalar(past[:, :], rel[:, :], float(W), FAR, ALU.is_ge, ALU.mult))
                ch.mark(dve.tensor_tensor(keyr[:, :], sbw[:, :], rel[:, :], ALU.add))
                ch.wait()
                dve.tensor_copy(srowr[:, :], lo32[:, :]).then_inc(keys, 1)
                dve.tensor_tensor(keyr[:, :], keyr[:, :], past[:, :], ALU.add).then_inc(keys, 1)
                dve.wait_ge(spans_T, 3)
                ch.mark(dve.tensor_copy(first[:, :], PS[0][0:1, 0:Q]))
                ch.mark(dve.tensor_reduce(fl[:, 0:1], PS[0][0:1, 128:128 + Q], AX.X, ALU.max))
                ch.mark(dve.tensor_reduce(fl[:, 1:2], PS[0][0:1, 256:256 + Q], AX.X, ALU.max))
                ch.wait()
                ch.mark(dve.tensor_copy(base_row[:, :], first[:, :]))
                ch.mark(dve.tensor_scalar(flag[:, 0:1], fl[:, 0:1], float(W), None, ALU.is_ge))
                dve.tensor_scalar(fl[:, 2:3], fl[:, 1:2], 0.0, -1.0, ALU.max, ALU.mult).then_inc(wmax, 1)
                for i, tab in enumerate((srow, key, wexp)):
                    dve.wait_ge(tables_T, i + 1)
                    dve.tensor_copy(tab[:, :, :], PS[1 + i][:, 0:SUB * Q].rearrange("p (j q) -> p q j", j=SUB)).then_inc(tables, 1)
                dve.wait_ge(weights, 2)
                for m in range(3):
                    ch.mark(dve.tensor_copy(part[:, :, m, :], wexp[:, :, :]))
                    if m < 2:
                        ch.wait()
                        ch.mark(dve.tensor_tensor(wexp[:, :, :], wexp[:, :, :], part[:, :, m, :], ALU.subtract))
                        ch.wait()

            @block.tensor
            def _(pe):
                pe.wait_ge(consts, 4)
                pe.wait_ge(spans, 1)
                for i in range(3):
                    pe.transpose(PS[0][0:1, 128 * i:128 * i + Q], est[:, i:i + 1], ident[0:Q, 0:Q]).then_inc(spans_T, 1)
                pe.wait_ge(keys, 2)
                for i, tab in enumerate((srowr, keyr, wrow)):
                    for j in range(SUB):
                        tr = pe.transpose(PS[1 + i][:, j * Q:(j + 1) * Q], tab[:, j * P:(j + 1) * P], ident[0:Q, 0:Q])
                    tr.then_inc(tables_T, 1)
                pe.wait_ge(wmax, 1)
                pe.matmul(PS[4][:, 0:1], ones[0:1, :], fl[:, 2:3], start=True, stop=True).then_inc(wmax_all, 1)

            @block.scalar
            def _(act):
                act.wait_ge(wmax_all, 1)
                act.copy(negmax[:, :], PS[4][:, 0:1]).then_inc(weights, 1)
                act.wait_ge(weights, 1)
                act.wait_ge(tables, 3)
                act.activation(wexp[:, :, :], wexp[:, :, :], ACT.Exp, bias=negmax[:, 0:1]).then_inc(weights, 1)

        def one_hot(dve, to, index, n):
            return dve.tensor_tensor(to, iota[:, 0:n, :], index.to_broadcast([P, n, SUB]), ALU.is_equal)

        def weigh(dve, to, hot, q):
            return dve.tensor_tensor(to, hot.unsqueeze(1).to_broadcast([P, 3, P, SUB]),
                                     part[:, ds(q, 1), :, :].rearrange("p a m j -> p (a m) j").unsqueeze(2).to_broadcast(
                                         [P, 3, P, SUB]), ALU.mult)

        def edge_product(pe, bank, rows, keys):
            n = rows.shape[1]
            for j in range(SUB):
                for m in range(n):
                    mm = pe.matmul(bank[:, 0:KW], rows[:, m, :, j], keys[:, :, j],
                                   start=(j == 0 and m == 0), stop=(j == SUB - 1 and m == n - 1))
            return mm

        def norm_phase(tag, Xn=None, XT=None, proj=None, sync=None, weights_in=None):
            with ExitStack() as ctx:
                staged = sb(ctx, "staged" + tag, [P, 2, D])
                turned = sb(ctx, "turned" + tag, [P, 2, KD, P])
                stat, root, inv, normed, xposed, saved, kept, mm, done = sems(
                    ctx, *(n + tag for n in ("stat", "root", "inv", "normed", "xposed", "turned", "kept", "proj_mm", "proj_done")))
                block = ctx.enter_context(nc.Block())
                if sync is not None:
                    block.sync(sync)

                @block.vector
                def _(dve):
                    for t in range(NT):
                        dve.bn_stats(stats[:, t, :], X[:, t, :]).then_inc(stat, 1)
                    for t in range(NT):
                        dve.wait_ge(stat, t + 1)
                        dve.bn_aggr(mv[:, t, :], stats[:, t, :]).then_inc(stat, 1)
                    dve.wait_ge(root, 1)
                    dve.reciprocal(rstd[:, :], std[:, :]).then_inc(inv, 1)
                    dve.wait_ge(inv, 1)

                    def pair(i):
                        for p in range(2):
                            t = 2 * i + p
                            after(dve, xposed, t - 1)
                            if Xn is not None:
                                after(dve, kept, t - 1)
                            dve.tensor_scalar(staged[:, p, :], tile_of(X, t), mv[:, ds(t, 1), 0], rstd[:, ds(t, 1)],
                                              ALU.subtract, ALU.mult).then_inc(normed, 1)
                    def close(i):
                        for p in range(2):
                            t = 2 * i + p
                            dve.wait_ge(mm, t + 1)
                            dve.tensor_tensor(tile_of(proj[2], t), PS[2 + p][:, 0:proj[0].shape[2]], proj[1],
                                              ALU.add).then_inc(done, 1)

                    pair(0)
                    with dve.Fori(1, NT // 2) as i:
                        pair(i)
                        if proj is not None:
                            close(i - 1)
                    if proj is not None:
                        close(NT // 2 - 1)

                @block.scalar
                def _(act):
                    act.wait_ge(stat, 2 * NT)
                    act.activation(std[:, :], mv[:, :, 1], ACT.Sqrt, bias=eps[:, 0:1]).then_inc(root, 1)

                    def pair(i):
                        for p in range(2):
                            t = 2 * i + p
                            act.wait_ge(xposed, t + 1)
                            src = PS[p][:, :].rearrange("p (k n) -> p k n", k=KD)
                            if XT is not None:
                                act.copy(XT[:, :, ds(t * P, P)], src).then_inc(saved, 1)
                            else:
                                after(act, mm, t - 1)
                                act.copy(turned[:, p, :, :], src).then_inc(saved, 1)
                    looped(act, NT // 2, pair)

                if Xn is not None:
                    @block.gpsimd
                    def _(pool):
                        def pair(i):
                            for p in range(2):
                                pool.wait_ge(normed, 2 * i + p + 1)
                                pool.tensor_copy(tile_of(Xn, 2 * i + p), staged[:, p, :]).then_inc(kept, 1)
                        looped(pool, NT // 2, pair)

                @block.tensor
                def _(pe):
                    if weights_in is not None:
                        pe.wait_ge(*weights_in)

                    def turn(t, p):
                        pe.wait_ge(normed, t + 1)
                        after(pe, saved, t - 1)
                        for k in range(KD):
                            tr = pe.transpose(PS[p][:, k * P:(k + 1) * P], staged[:, p, k * P:(k + 1) * P], ident[:, :])
                        tr.then_inc(xposed, 1)

                    def pair(i):
                        for p in range(2):
                            t = 2 * i + p
                            turn(t, p)
                            if proj is not None:
                                pe.wait_ge(saved, t + 1)
                                after(pe, done, t - 1)
                                n = proj[0].shape[2]
                                for k in range(KD):
                                    m = pe.matmul(PS[2 + p][:, 0:n], turned[:, p, k, :], proj[0][:, k, :],
                                                  start=(k == 0), stop=(k == KD - 1))
                                m.then_inc(mm, 1)
                    looped(pe, NT // 2, pair)

        class Graph:

            def __init__(self, ctx, tag, dst, weighted, banks):
                self.dst, self.weighted, self.banks = dst, weighted, banks
                self.hot_key = sb(ctx, "hot_key" + tag, [P, 2, KW, SUB], BF16)
                self.hot_src = sb(ctx, "hot_src" + tag, [P, 2, P, SUB], BF16)
                self.hot_w = sb(ctx, "hot_w" + tag, [P, 2, 3, P, SUB], BF16) if weighted else None
                self.rows, self.hot, self.cells, self.added = sems(
                    ctx, *(n + tag for n in ("hot_rows", "hot", "cells", "added")))

            def make(self, dve, q, p):
                after(dve, self.cells, q - 1)
                one_hot(dve, self.hot_src[:, p, :, :], srow[:, ds(q, 1), :], P).then_inc(self.rows, 1)
                hk = one_hot(dve, self.hot_key[:, p, :, :], key[:, ds(q, 1), :], KW)
                if self.weighted:
                    dve.wait_ge(self.rows, q + 1)
                    hk = weigh(dve, self.hot_w[:, p, :, :, :], self.hot_src[:, p, :, :], q)
                hk.then_inc(self.hot, 1)

            def add(self, dve, q, p):
                base = dve.value_load(base_row[0:1, ds(q, 1)], min_val=0, max_val=NP)
                dve.wait_ge(self.cells, q + 1)
                after(dve, self.added, q)
                window = self.dst[:, :, ds(base, W)]
                dve.tensor_tensor(window, window, self.banks[p][:, 0:KW].rearrange("p (b w) -> p b w", w=W),
                                  ALU.add).then_inc(self.added, 1)

            def build(self, dve):
                self.make(dve, 0, 0)
                self.make(dve, 1, 1)
                self.add(dve, 0, 0)
                self.make(dve, 2, 0)
                self.add(dve, 1, 1)
                with dve.Fori(1, Q // 2 - 1) as i:
                    self.make(dve, 2 * i + 1, 1)
                    self.add(dve, 2 * i, 0)
                    self.make(dve, 2 * i + 2, 0)
                    self.add(dve, 2 * i + 1, 1)
                self.make(dve, Q - 1, 1)
                self.add(dve, Q - 2, 0)
                self.add(dve, Q - 1, 1)

            def sums(self, dve, q, n, last=False):
                for i in range(n):
                    if not (last and i == n - 1):
                        self.make(dve, q + (i + 1), (i + 1) % 2)
                    self.add(dve, q + i, i % 2)

            def products(self, pe, q, n):
                for i in range(n):
                    self.multiply(pe, q + i, i % 2)

            def multiply(self, pe, q, p):
                pe.wait_ge(self.hot, q + 1)
                after(pe, self.added, q - 1)
                mm = edge_product(pe, self.banks[p], self.hot_w[:, p, :, :, :] if self.weighted else
                                  self.hot_src[:, p, :, :].unsqueeze(1), self.hot_key[:, p, :, :])
                mm.then_inc(self.cells, 1)

        def general_passes(tag, dst, weighted):
            with ExitStack() as ctx:
                hot_key = sb(ctx, "ghot_key" + tag, [P, KW, SUB], BF16)
                hot_src = sb(ctx, "ghot_src" + tag, [P, P, SUB], BF16)
                hot_w = sb(ctx, "ghot_w" + tag, [P, 3, P, SUB], BF16) if weighted else None
                relp = sb(ctx, "relp" + tag, [Q, CE])
                keyp = sb(ctx, "keyp" + tag, [Q, CE])
                past = sb(ctx, "pastp" + tag, [Q, CE])
                keycol = sb(ctx, "keycol" + tag, [P, Q, SUB], BF16)
                firstp = sb(ctx, "firstp" + tag, [1, Q])
                basep = sb(ctx, "basep" + tag, [1, Q], I32)
                step, keys, keys_T, rows, hot, cells, added = sems(
                    ctx, *(n + tag for n in ("gstep", "gkeys", "gkeys_T", "grows", "ghot", "gcells", "gadded")))
                block = ctx.enter_context(nc.Block())
                SP_ = 7

                @block.vector
                def _(dve):
                    wide = dve.value_load(flag[0:1, 0:1], min_val=0, max_val=1)
                    with dve.If(wide > 0):
                        ch = Chain(dve, step)
                        ch.mark(dve.tensor_copy(relp[:, :], rel[:, :]))
                        ch.mark(dve.tensor_copy(firstp[:, :], first[:, :]))
                        with dve.Fori(0, PASSES - 1) as n:
                            ch.at(n * SP_ + 2)
                            ch.wait()
                            ch.mark(dve.tensor_scalar(relp[:, :], relp[:, :], float(W), None, ALU.subtract))
                            ch.mark(dve.tensor_scalar(firstp[:, :], firstp[:, :], float(W), float(NP), ALU.add, ALU.min))
                            ch.wait()
                            ch.mark(dve.tensor_copy(basep[:, :], firstp[:, :]))
                            ch.mark(dve.tensor_scalar(past[:, :], relp[:, :], float(W), FAR, ALU.is_ge, ALU.mult))
                            ch.mark(dve.tensor_tensor(keyp[:, :], sbw[:, :], relp[:, :], ALU.add))
                            ch.wait()
                            ch.mark(dve.tensor_tensor(keyp[:, :], keyp[:, :], past[:, :], ALU.add))
                            ch.wait()
                            ch.mark(dve.tensor_scalar(past[:, :], relp[:, :], 0.0, FAR, ALU.is_lt, ALU.mult))
                            ch.wait()
                            assert ch.n == SP_
                            dve.tensor_tensor(keyp[:, :], keyp[:, :], past[:, :], ALU.add).then_inc(keys, 1)
                            dve.wait_ge(keys_T, n + 1)
                            dve.tensor_copy(keycol[:, :, :],
                                            PS[1][:, 0:SUB * Q].rearrange("p (j q) -> p q j", j=SUB)).then_inc(keys, 1)
                            with dve.Fori(0, Q) as q:
                                dve.wait_ge(keys, 2 * n + 2)
                                one_hot(dve, hot_src[:, :, :], srow[:, ds(q, 1), :], P).then_inc(rows, 1)
                                h = one_hot(dve, hot_key[:, :, :], keycol[:, ds(q, 1), :], KW)
                                if weighted:
                                    dve.wait_ge(rows, n * Q + q + 1)
                                    h = weigh(dve, hot_w[:, :, :, :], hot_src[:, :, :], q)
                                h.then_inc(hot, 1)
                                base = dve.value_load(basep[0:1, ds(q, 1)], min_val=0, max_val=NP)
                                dve.wait_ge(cells, n * Q + q + 1)
                                window = dst[:, :, ds(base, W)]
                                dve.tensor_tensor(window, window, PS[0][:, 0:KW].rearrange("p (b w) -> p b w", w=W),
                                                  ALU.add).then_inc(added, 1)
                                dve.wait_ge(added, n * Q + q + 1)

                @block.tensor
                def _(pe):
                    wide = pe.value_load(flag[0:1, 0:1], min_val=0, max_val=1)
                    with pe.If(wide > 0):
                        with pe.Fori(0, PASSES - 1) as n:
                            pe.wait_ge(keys, 2 * n + 1)
                            for j in range(SUB):
                                tr = pe.transpose(PS[1][:, j * Q:(j + 1) * Q], keyp[:, j * P:(j + 1) * P], ident[0:Q, 0:Q])
                            tr.then_inc(keys_T, 1)
                            with pe.Fori(0, Q) as q:
                                pe.wait_ge(hot, n * Q + q + 1)
                                mm = edge_product(pe, PS[0], hot_w[:, :, :, :] if weighted else hot_src[:, :, :].unsqueeze(1),
                                                  hot_key[:, :, :])
                                mm.then_inc(cells, 1)

        with ExitStack() as g1:
            XT = sb(g1, "XT1", [P, KD, NP])
            C = sb(g1, "C", [P, NT, CW])
            Xn = [sb(g1, f"Xn{i}", [P, NT, D]) for i in range(2)]
            G = sb(g1, "G", [P, KD, NP])
            w_gate = sb(g1, "w_gate", [P, KD, D])
            w_gnn = sb(g1, "w_gnn", [P, KD, D])
            zeros = sb(g1, "zeros", [P, D])
            zeroed, = sems(g1, "zeroed")
            gw_in, gwr_in = sems(g1, "gnn_w_in", "gate_w_in")
            norm_phase("1", Xn=Xn[0], XT=XT)

            def gate_pe(pe, wait_input, gate_mm, gated, c, g):
                wait_input(c)
                after(pe, gated, KD * c + g - 1)
                bank = PS[4 + g % 2][:, 0:CH]
                for k in range(KD):
                    m = pe.matmul(bank, w_gate[:, k, g * P:(g + 1) * P], XT[:, k, ds(c * CH, CH)],
                                  start=(k == 0), stop=(k == KD - 1))
                m.then_inc(gate_mm, 1)

            def gate_act(act, gate_mm, gated, c, g, col):
                act.wait_ge(gate_mm, 4 * c + g + 1)
                bank = PS[4 + g % 2][:, 0:CH]
                act.activation(G[:, g, ds(c * CH, CH)], bank, ACT.Sigmoid, bias=bcol[:, col + g:col + g + 1]).then_inc(gated, 1)

            with ExitStack() as ctx:
                cleared, gate_mm, gated = sems(ctx, "cleared_c", "gate_mm1", "gated1")
                graph = Graph(ctx, "_c", C, False, (PS[2], PS[3]))
                block = ctx.enter_context(nc.Block())

                @block.sync
                def _(sp):
                    sp.dma_start(w_gate[:, :, :], a["gate_w1"].rearrange("(k p) g -> p k g", p=P)).then_inc(gwr_in, 16)
                    sp.dma_start(w_gnn[:, :, :], a["gnn_w1"].rearrange("(k p) g -> p k g", p=P)).then_inc(gw_in, 16)
                    sp.wait_ge(zeroed, 1)
                    for b in range(2):
                        sp.dma_start(routed[b].rearrange("(t p) d -> p t d", p=P),
                                     zeros[:, :].unsqueeze(1).to_broadcast([P, ST, D])).then_inc(cleared_slots, 16)

                @block.gpsimd
                def _(pool):
                    pool.memset(C[:, :, :], 0.0).then_inc(cleared, 1)
                    pool.memset(zeros[:, :], 0.0).then_inc(zeroed, 1)

                @block.vector
                def _(dve):
                    dve.wait_ge(cleared, 1)
                    graph.build(dve)

                @block.scalar
                def _(act):
                    def chunk(c):
                        for g in range(KD):
                            gate_act(act, gate_mm, gated, c, g, BIAS_COLS["gnn_br1"])
                    looped(act, NC, chunk)

                @block.tensor
                def _(pe):
                    pe.wait_ge(gwr_in, 16)

                    def chunk(c):
                        for g in range(KD):
                            graph.multiply(pe, 8 * c + 2 * g, 0)
                            graph.multiply(pe, 8 * c + 2 * g + 1, 1)
                            gate_pe(pe, lambda c: None, gate_mm, gated, c, g)
                    looped(pe, NC, chunk)
                    with pe.Fori(NC * KD, Q // 2) as i:
                        graph.multiply(pe, 2 * i, 0)
                        graph.multiply(pe, 2 * i + 1, 1)
            general_passes("_c", C, False)

            with ExitStack() as ctx:
                dis_all = sb(g1, "dis_all", [P, NP])
                dis_col = sb(g1, "dis_col", [P, NT])
                Y = sb(g1, "Y", [P, KD, CH])
                H = sb(g1, "H", [P, KD, CH])
                mix = sb(g1, "mix", [P, KD, CH])
                (loops, deg_mm, deg_root, dis_ready, col_mm, scaled) = sems(
                    ctx, "self_loops", "deg_mm", "deg_root", "dis_ready", "dis_col_mm", "scaled")
                block = ctx.enter_context(nc.Block())

                @block.vector
                def _(dve):
                    for t in range(NT):
                        diag = C[:, t, t * P:(t + 1) * P]
                        dve.tensor_tensor(diag, diag, ident[:, :], ALU.add).then_inc(loops, 1)

                    def chunk(c):
                        dve.wait_ge(deg_root, c + 1)
                        dve.reciprocal(dis_all[:, ds(c * CH, CH)], dis_all[:, ds(c * CH, CH)]).then_inc(dis_ready, 1)
                    looped(dve, NC, chunk)
                    dve.wait_ge(col_mm, 1)
                    dve.tensor_copy(dis_col[:, :], PS[2][:, 0:NT]).then_inc(dis_ready, 1)
                    dve.wait_ge(dis_ready, NC + 1)
                    for t in range(NT):
                        dve.tensor_scalar(Xn[0][:, t, :], Xn[0][:, t, :], dis_col[:, t:t + 1], None, ALU.mult).then_inc(scaled, 1)

                @block.tensor
                def _(pe):
                    pe.wait_ge(loops, NT)

                    def chunk(c):
                        after(pe, deg_root, c)
                        for s in range(NT):
                            m = pe.matmul(PS[0][:, 0:CH], ones[:, :], C[:, s, ds(c * CH, CH)], start=(s == 0), stop=(s == NT - 1))
                        m.then_inc(deg_mm, 1)
                    looped(pe, NC, chunk)
                    pe.wait_ge(dis_ready, NC)
                    for t in range(NT):
                        m = pe.matmul(PS[2][:, t:t + 1], dis_all[0:1, t * P:(t + 1) * P], ones[0:1, 0:1], start=True, stop=True)
                    m.then_inc(col_mm, 1)

                @block.scalar
                def _(act):
                    def chunk(c):
                        act.wait_ge(deg_mm, c + 1)
                        act.activation(dis_all[:, ds(c * CH, CH)], PS[0][:, 0:CH], ACT.Sqrt).then_inc(deg_root, 1)
                    looped(act, NC, chunk)

            with ExitStack() as ctx:
                mm_y, y_done, mm_o, mixed, relu, saved, turn, turned, gate_mm, gated = zip(*[
                    sems(ctx, *(f"{n}{l}" for n in ("agg_mm", "y_done", "out_mm", "mix_step", "relu_done", "h_saved",
                                                    "h_turn", "h_turned", "l_gate_mm", "l_gated"))) for l in range(2)])
                w2_in, = sems(ctx, "layer2_w_in")
                block = ctx.enter_context(nc.Block())
                MIX = 6

                @block.sync
                def _(sp):
                    sp.wait_ge(gw_in, 16)
                    sp.dma_start(w_gate[:, :, :], a["gate_w2"].rearrange("(k p) g -> p k g", p=P)).then_inc(w2_in, 16)
                    sp.wait_ge(mm_o[0], KD * NC)
                    sp.dma_start(w_gnn[:, :, :], a["gnn_w2"].rearrange("(k p) g -> p k g", p=P)).then_inc(gw_in, 16)

                @block.tensor
                def _(pe):
                    def aggregate(l, c):
                        for f in range(KD):
                            bank = PS[f % 2][:, 0:CH]
                            after(pe, y_done[l], KD * c + f - 1)
                            for s in range(NT):
                                m = pe.matmul(bank, Xn[l][:, s, f * P:(f + 1) * P], C[:, s, ds(c * CH, CH)],
                                              start=(s == 0), stop=(s == NT - 1))
                            m.then_inc(mm_y[l], 1)

                    def project(l, c):
                        pe.wait_ge(y_done[l], KD * (c + 1))
                        for g in range(KD):
                            bank = PS[2 + g % 2][:, 0:CH]
                            after(pe, mixed[l], MIX * c + g - 1 if g > 1 else MIX * (c - 1) + g + 3)
                            for k in range(KD):
                                m = pe.matmul(bank, w_gnn[:, k, g * P:(g + 1) * P], Y[:, k, :], start=(k == 0), stop=(k == KD - 1))
                            m.then_inc(mm_o[l], 1)

                    def turn_back(l, c):
                        pe.wait_ge(relu[l], c + 1)
                        for j in range(TPC):
                            after(pe, turned[l], TPC * (c - 1) + j + 1)
                            for f in range(KD):
                                m = pe.transpose(PS[6 + j][:, f * P:(f + 1) * P], H[:, f, j * P:(j + 1) * P], ident[:, :])
                            m.then_inc(turn[l], 1)

                    for l in range(2):
                        pe.wait_ge(gw_in, 16 * (l + 1))
                        aggregate(l, 0)
                        project(l, 0)
                        aggregate(l, 1)
                        turn_back(l, 0)
                        project(l, 1)
                        with pe.Fori(2, NC) as c:
                            aggregate(l, c)
                            turn_back(l, c - 1)
                            project(l, c)
                        if l == 0:
                            pe.wait_ge(w2_in, 16)
                            for c in range(NC - 1):
                                for g in range(KD):
                                    gate_pe(pe, lambda c: pe.wait_ge(saved[0], c + 1), gate_mm[0], gated[0], c, g)
                            turn_back(l, NC - 1)
                            for g in range(KD):
                                gate_pe(pe, lambda c: pe.wait_ge(saved[0], c + 1), gate_mm[0], gated[0], NC - 1, g)
                            pe.wait_ge(turned[0], NT)
                        else:
                            turn_back(l, NC - 1)

                @block.vector
                def _(dve):
                    def y_out(l, c):
                        for f in range(KD):
                            dve.wait_ge(mm_y[l], KD * c + f + 1)
                            dve.tensor_tensor(Y[:, f, :], PS[f % 2][:, 0:CH],
                                              dis_all[:, ds(c * CH, CH)], ALU.mult).then_inc(y_done[l], 1)

                    def mix_out(l, c):
                        ch = Chain(dve, mixed[l])
                        ch.at(MIX * c)
                        col = BIAS_COLS["gnn_b1" if l == 0 else "gnn_b2"]
                        for g in range(KD):
                            dve.wait_ge(mm_o[l], KD * c + g + 1)
                            after(dve, relu[l], c)
                            ch.mark(dve.scalar_tensor_tensor(
                                out=mix[:, g, :], in0=PS[2 + g % 2][:, 0:CH],
                                scalar=bcol[:, col + g:col + g + 1], in1=XT[:, g, ds(c * CH, CH)],
                                op0=ALU.add, op1=ALU.subtract))
                        ch.wait()
                        if l == 1:
                            dve.wait_ge(gated[0], KD * (c + 1))
                        ch.mark(dve.tensor_tensor(mix[:, :, :], mix[:, :, :], G[:, :, ds(c * CH, CH)], ALU.mult))
                        ch.wait()
                        ch.mark(dve.tensor_tensor(mix[:, :, :], mix[:, :, :], XT[:, :, ds(c * CH, CH)], ALU.add))
                        assert ch.n == MIX

                    def back(l, c):
                        for j in range(TPC):
                            t = TPC * c + j
                            dve.wait_ge(turn[l], TPC * c + j + 1)
                            if l == 0:
                                dve.tensor_scalar(tile_of(Xn[1], t), PS[6 + j][:, :], dis_col[:, ds(t, 1)], None,
                                                  ALU.mult).then_inc(turned[l], 1)
                            else:
                                dve.tensor_tensor(tile_of(X, t), tile_of(X, t), PS[6 + j][:, :], ALU.add).then_inc(turned[l], 1)

                    for l in range(2):
                        y_out(l, 0)
                        mix_out(l, 0)
                        with dve.Fori(1, NC) as c:
                            y_out(l, c)
                            back(l, c - 1)
                            mix_out(l, c)
                        back(l, NC - 1)

                @block.scalar
                def _(act):
                    def chunk(l, c):
                        act.wait_ge(mixed[l], MIX * c + MIX)
                        after(act, turn[l], TPC * c)
                        if l == 0:
                            act.activation(XT[:, :, ds(c * CH, CH)], mix[:, :, :], ACT.Relu).then_inc(saved[l], 1)
                        act.activation(H[:, :, :], mix[:, :, :], ACT.Relu).then_inc(relu[l], 1)
                    chunk(0, 0)
                    with act.Fori(1, NC) as c:
                        chunk(0, c)
                    for c in range(NC):
                        for g in range(KD):
                            gate_act(act, gate_mm[0], gated[0], c, g, BIAS_COLS["gnn_br2"])
                    chunk(1, 0)
                    with act.Fori(1, NC) as c:
                        chunk(1, c)
        nc.gpsimd.sem_clear(range(first_reused, w2_in.num + 1))
        nc.all_engine_barrier()

        A = sb(top, "A", [P, NT, CW])
        with ExitStack() as g2:
            FIRST_Q, SHARED_Q, TILE_Q = 2, 8, 2
            _left = Q - FIRST_Q - SHARED_Q * (NC - 1) - 2 * TILE_Q * (ST - 2)
            assert _left >= 0 and _left % 2 == 0
            BANK_Q = _left - _left // 4 * 2, _left // 4 * 2
            q_bank = [FIRST_Q + SHARED_Q * (NC - 1)]
            q_bank.append(q_bank[0] + BANK_Q[0] + TILE_Q * (ST - 2))
            graph = Graph(g2, "_a", A, True, (PS[0], PS[1]))
            a_cleared, = sems(g2, "a_cleared")
            slot = sb(g2, "slot", [P, 2 * NT], I32)
            gate = sb(g2, "gate", [P, 2 * NT])
            tile_expert = sb(g2, "tile_expert", [1, 2 * ST], I32)
            gated_hot = sb(g2, "gated_hot", [32, NP])
            bias2 = sb(g2, "bias2", [2 * NE + 1, D])
            W1 = [sb(g2, "W1_0", [P, NE * KD * FF]), None]
            w1_in, w2_in, scattered, bias2_in = sems(g2, "expert_w1_in", "expert_w2_in", "scattered", "bias2_in")

            def load_w1(sp, b):
                tag = ("sp", "fq")[b]
                for e in range(NE):
                    sp.dma_start(W1[b][:, e * KD * FF:(e + 1) * KD * FF].rearrange("p (k f) -> p k f", k=KD),
                                 a[f"W1_{tag}"][e].rearrange("(k p) f -> p k f", p=P)).then_inc(w1_in, 16)

            def load_w2(sp, b, W2):
                tag = ("sp", "fq")[b]
                for e in range(NE):
                    sp.dma_start(W2[:, e * 2 * D:(e + 1) * 2 * D].rearrange("p (f d) -> p f d", f=2),
                                 a[f"W2_{tag}"][e].rearrange("(f p) d -> p f d", p=P)).then_inc(w2_in, 16)

            with ExitStack() as ctx2:
                XT = sb(ctx2, "XT2", [P, KD, NP])
                Xn = sb(ctx2, "Xn2", [P, NT, D])

                def early(sp):
                    load_w1(sp, 0)
                norm_phase("2", Xn=Xn, XT=XT, sync=early)

                ws1 = sb(ctx2, "ws1", [P, KD, FF])
                ws2 = sb(ctx2, "ws2", [P, 2, D])
                wr = sb(ctx2, "wr", [P, KD, 2 * NE])
                br = sb(ctx2, "br", [2 * NE, 1])
                LT = sb(ctx2, "LT", [2 * NE, NP])
                HS = sb(ctx2, "HS", [P, 2, CH])
                L = sb(ctx2, "L", [P, 2 * NT, NE])
                ex = sb(ctx2, "ex", [P, 2 * NT, NE])
                hotx = sb(ctx2, "hotx", [P, 2 * NT, NE])
                col = sb(ctx2, "col", [P, 4, 2 * NT])
                rev = sb(ctx2, "rev", [P, NE])
                real = sb(ctx2, "real", [P, 1])
                tri = sb(ctx2, "tri", [P, P])
                run = sb(ctx2, "run", [P, NT + 1, 2 * NE])
                thresholds = sb(ctx2, "thresholds", [P, NT])
                tiles_gt = sb(ctx2, "tiles_gt", [P, 2 * NE, NT])
                tiles = sb(ctx2, "tiles", [P, 2, NE])
                start = sb(ctx2, "start", [P, 2, NE + 1])
                start_row = sb(ctx2, "start_row", [P, 2 * NE])
                slotf = sb(ctx2, "slotf", [P, 2 * NT])
                tile_no = sb(ctx2, "tile_no", [1, ST])
                past = sb(ctx2, "pastt", [1, ST, NE])
                chosen = sb(ctx2, "chosen", [1, 2, ST])
                (sw_in, rmm, routed_T, rT, lt, step, expd, hot_ready, prefix, slots_ready, ghot_T, ghot, s1, hs, s2, xadd,
                 rconst, tri1) = sems(
                    ctx2, "shared_w_in", "router_mm", "logits_T", "logits_turned", "logits", "route_step", "route_exp",
                    "hot_ready", "prefix_mm", "slots_ready", "gated_hot_T", "gated_hot_saved", "shared1_mm", "shared_h",
                    "shared2_mm", "shared_added", "route_consts", "tri_ones")
                block = ctx2.enter_context(nc.Block())

                @block.sync
                def _(sp):
                    sp.dma_start(wr[:, :, :], a["router_w"].rearrange("(k p) e -> p k e", p=P)).then_inc(sw_in, 16)
                    sp.dma_start(br[:, :], a["router_b"]).then_inc(sw_in, 16)
                    sp.dma_start(ws1[:, :, :], a["ws1"].rearrange("(k p) f -> p k f", p=P)).then_inc(sw_in, 16)
                    sp.dma_start(ws2[:, :, :], a["ws2"].rearrange("(f p) d -> p f d", p=P)).then_inc(sw_in, 16)
                    sp.dma_start(bias2[:, :], a["b2_all"]).then_inc(bias2_in, 16)

                @block.gpsimd
                def _(pool):
                    pool.memset(tri[:, :], 1.0).then_inc(tri1, 1)
                    pool.iota(rev[:, :], pattern=[[-1, NE]], base=NE, channel_multiplier=0,
                              allow_small_or_imprecise_dtypes=True).then_inc(rconst, 1)
                    pool.memset(real[:, :], 1.0).then_inc(tri1, 1)
                    pool.iota(thresholds[:, :], pattern=[[P, NT]], base=0, channel_multiplier=0,
                              allow_small_or_imprecise_dtypes=True).then_inc(rconst, 1)
                    pool.iota(tile_no[:, :], pattern=[[1, ST]], base=0, channel_multiplier=0,
                              allow_small_or_imprecise_dtypes=True).then_inc(rconst, 1)
                    pool.memset(gated_hot[:, :], 1.0).then_inc(rconst, 1)
                    pool.memset(run[:, 0, :], 0.0).then_inc(rconst, 1)
                    pool.memset(start[:, :, :], 0.0).then_inc(rconst, 1)
                    pool.wait_ge(tri1, 2)
                    pool.affine_select(out=tri[:, :], in_=tri[:, :], compare_op=ALU.is_ge, fill=0.0, base=-1,
                                       pattern=[[1, P]], channel_multiplier=-1).then_inc(rconst, 1)
                    pool.affine_select(out=real[:, :], in_=real[:, :], compare_op=ALU.is_ge, fill=0.0, base=LAST - 1,
                                       pattern=[[0, 1]], channel_multiplier=-1).then_inc(rconst, 1)
                    pool.memset(A[:, :, :], 0.0).then_inc(a_cleared, 1)
                    pool.wait_ge(slots_ready, 1)
                    pool.wait_ge(cleared_slots, 32)
                    for t in range(NT):
                        n = P if t < NT - 1 else LAST
                        for b in range(2):
                            pool.indirect_dma_start(
                                routed[b], bass.IndirectOffsetOnAxis(ap=slot[0:n, 2 * t + b:2 * t + b + 1], axis=0),
                                Xn[0:n, t, :], None).then_inc(scattered, 16)
                    pool.wait_ge(scattered, 2 * NT * 16)

                @block.tensor
                def _(pe):
                    pe.wait_ge(sw_in, 64)

                    def router(c):
                        after(pe, lt, c)
                        for k in range(KD):
                            m = pe.matmul(PS[0][0:2 * NE, 0:CH], wr[:, k, :], XT[:, k, ds(c * CH, CH)],
                                          start=(k == 0), stop=(k == KD - 1))
                        m.then_inc(rmm, 1)
                    looped(pe, NC, router)
                    pe.wait_ge(lt, NC)
                    for t in range(NT):
                        m = pe.transpose(PS[1][:, 2 * NE * t:2 * NE * (t + 1)], LT[:, t * P:(t + 1) * P], ident[0:2 * NE, 0:2 * NE])
                    m.then_inc(rT, 1)

                    def shared(c):
                        after(pe, hs, 2 * c)
                        for f in range(2):
                            for k in range(KD):
                                m = pe.matmul(PS[2 + f][:, 0:CH], ws1[:, k, f * P:(f + 1) * P], XT[:, k, ds(c * CH, CH)],
                                              start=(k == 0), stop=(k == KD - 1))
                            m.then_inc(s1, 1)
                        pe.wait_ge(hs, 2 * c + 2)
                        for j in range(TPC):
                            after(pe, xadd, TPC * (c - 1) + j + 1 if isinstance(c, int) else TPC * c + (j + 1 - TPC))
                            for f in range(2):
                                m = pe.matmul(PS[4 + j][:, :], HS[:, f, j * P:(j + 1) * P], ws2[:, f, :],
                                              start=(f == 0), stop=(f == 1))
                            m.then_inc(s2, 1)
                    shared(0)
                    pe.wait_ge(hot_ready, 1)
                    flat = hotx[:, :, :].rearrange("p t e -> p (t e)")
                    pe.matmul(PS[6][:, 0:2 * NT * NE], tri[:, :], flat, start=True, stop=True).then_inc(prefix, 1)
                    pe.matmul(PS[7][:, 0:2 * NT * NE], ones[:, :], flat, start=True, stop=True).then_inc(prefix, 1)
                    graph.products(pe, 0, FIRST_Q)
                    with pe.Fori(1, NC) as c:
                        shared(c)
                        graph.products(pe, SHARED_Q * c + (FIRST_Q - SHARED_Q), SHARED_Q)
                    pe.wait_ge(ghot_T, 1)
                    pe.wait_ge(graph.added, q_bank[0])
                    for t in range(NT):
                        bank = t // 4
                        m = pe.transpose(PS[(0, 1, 6)[bank]][0:2 * NE, (t % 4) * P:(t % 4 + 1) * P],
                                         ex[:, 2 * t:2 * t + 2, :].rearrange("p t e -> p (t e)"), ident[:, :])
                    m.then_inc(routed_T, 1)

                @block.scalar
                def _(act):
                    def logits(c):
                        act.wait_ge(rmm, c + 1)
                        act.activation(LT[:, ds(c * CH, CH)], PS[0][0:2 * NE, 0:CH], ACT.Identity, bias=br[:, 0:1]).then_inc(lt, 1)
                    looped(act, NC, logits)

                    def shared(c):
                        for f in range(2):
                            act.wait_ge(s1, 2 * c + f + 1)
                            after(act, s2, TPC * c)
                            act.activation(HS[:, f, :], PS[2 + f][:, 0:CH], ACT.Gelu,
                                           bias=bcol[:, BIAS_COLS["bs1"] + f:BIAS_COLS["bs1"] + f + 1]).then_inc(hs, 1)
                    act.wait_ge(expd, 1)
                    act.activation(ex[:, :, :], L[:, :, :], ACT.Exp).then_inc(expd, 1)
                    looped(act, NC, shared)
                    act.wait_ge(routed_T, 1)
                    for i, bank in enumerate((0, 1, 6)):
                        w = min(4, NT - 4 * i) * P
                        act.copy(gated_hot[0:2 * NE, 4 * i * P:4 * i * P + w], PS[bank][0:2 * NE, 0:w]).then_inc(ghot, 1)

                @block.vector
                def _(dve):
                    ch = Chain(dve, step)
                    tt, tsc = dve.tensor_tensor, dve.tensor_scalar

                    def over(c2):
                        return c2.unsqueeze(2).to_broadcast([P, 2 * NT, NE])
                    dve.wait_ge(rT, 1)
                    dve.wait_ge(rconst, 8)
                    ch.mark(dve.tensor_copy(L[:, :, :], PS[1][:, 0:2 * NT * NE].rearrange("p (t e) -> p t e", e=NE)))
                    ch.wait()
                    ch.mark(dve.tensor_reduce(col[:, 0, :], L[:, :, :], AX.X, ALU.max))
                    ch.wait()
                    tt(L[:, :, :], L[:, :, :], over(col[:, 0, :]), ALU.subtract).then_inc(expd, 1)
                    dve.wait_ge(expd, 2)
                    ch.mark(dve.tensor_reduce(col[:, 1, :], ex[:, :, :], AX.X, ALU.add))
                    ch.mark(dve.tensor_reduce(col[:, 2, :], ex[:, :, :], AX.X, ALU.max))
                    ch.wait()
                    ch.mark(dve.reciprocal(gate[:, :], col[:, 1, :]))
                    ch.mark(tt(L[:, :, :], ex[:, :, :], over(col[:, 2, :]), ALU.is_equal))
                    ch.wait()
                    ch.mark(tt(gate[:, :], gate[:, :], col[:, 2, :], ALU.mult))
                    ch.mark(tt(L[:, :, :], L[:, :, :], rev[:, :].unsqueeze(1).to_broadcast([P, 2 * NT, NE]), ALU.mult))
                    ch.wait()
                    ch.mark(dve.tensor_reduce(col[:, 3, :], L[:, :, :], AX.X, ALU.max))
                    ch.wait()
                    ch.mark(tt(hotx[:, :, :], L[:, :, :], over(col[:, 3, :]), ALU.is_equal))
                    ch.wait()
                    tsc(hotx[:, 2 * NT - 2:2 * NT, :], hotx[:, 2 * NT - 2:2 * NT, :], real[:, 0:1], None, ALU.mult).then_inc(hot_ready, 1)
                    dve.wait_ge(hot_ready, 1)
                    tt(ex[:, :, :], hotx[:, :, :], over(gate[:, :]), ALU.mult).then_inc(ghot_T, 1)
                    dve.wait_ge(prefix, 2)
                    for t in range(NT):
                        ch.mark(tt(run[:, t + 1, :], run[:, t, :], PS[7][:, 2 * NE * t:2 * NE * (t + 1)], ALU.add))
                        ch.wait()
                    ch.mark(tt(tiles_gt[:, :, :], run[:, NT, :].unsqueeze(2).to_broadcast([P, 2 * NE, NT]),
                               thresholds[:, :].unsqueeze(1).to_broadcast([P, 2 * NE, NT]), ALU.is_gt))
                    ch.wait()
                    ch.mark(dve.tensor_reduce(tiles[:, :, :].rearrange("p b e -> p (b e)"), tiles_gt[:, :, :], AX.X, ALU.add))
                    for e in range(NE):
                        ch.wait()
                        ch.mark(tt(start[:, :, e + 1], start[:, :, e], tiles[:, :, e], ALU.add))
                    ch.wait()
                    ch.mark(tsc(start_row[:, :].rearrange("p (b e) -> p b e", b=2), start[:, :, 0:NE], float(P), None, ALU.mult))
                    Lv = L[:, :, :].rearrange("p (t b) e -> p t (b e)", b=2)
                    ch.mark(tt(Lv, PS[6][:, 0:2 * NT * NE].rearrange("p (t e) -> p t e", t=NT), run[:, 0:NT, :], ALU.add))
                    ch.wait()
                    ch.mark(tt(Lv, Lv, start_row[:, :].unsqueeze(1).to_broadcast([P, NT, 2 * NE]), ALU.add))
                    ch.wait()
                    ch.mark(tt(L[:, :, :], L[:, :, :], hotx[:, :, :], ALU.mult))
                    ch.wait()
                    ch.mark(dve.tensor_reduce(slotf[:, :], L[:, :, :], AX.X, ALU.add))
                    ch.wait()
                    dve.tensor_copy(slot[:, :], slotf[:, :]).then_inc(slots_ready, 1)
                    for b in range(2):
                        ch.mark(tt(past[:, :, :], tile_no[:, :].unsqueeze(2).to_broadcast([1, ST, NE]),
                                   start[0:1, b, 1:NE + 1].unsqueeze(1).to_broadcast([1, ST, NE]), ALU.is_ge))
                        ch.wait()
                        ch.mark(dve.tensor_reduce(chosen[:, b, :], past[:, :, :], AX.X, ALU.add))
                        ch.wait()
                    ch.mark(tsc(tile_expert[:, :], chosen[:, :, :].rearrange("p b t -> p (b t)"), float(NE - 1), None, ALU.min))
                    ch.wait()

                    def shared(c):
                        for j in range(TPC):
                            dve.wait_ge(s2, TPC * c + j + 1)
                            x_t = tile_of(X, TPC * c + j)
                            tt(x_t, x_t, PS[4 + j][:, :], ALU.add).then_inc(xadd, 1)
                    graph.make(dve, 0, 0)
                    shared(0)
                    dve.wait_ge(a_cleared, 1)
                    graph.sums(dve, 0, FIRST_Q)
                    with dve.Fori(1, NC) as c:
                        shared(c)
                        graph.sums(dve, SHARED_Q * c + (FIRST_Q - SHARED_Q), SHARED_Q)

            with ExitStack() as ctx2:
                W1[1] = sb(ctx2, "W1_1", [P, NE * KD * FF])
                W2 = sb(ctx2, "W2", [P, NE * 2 * D])
                graph.banks = PS[4], PS[5]
                xg = sb(ctx2, "xg", [P, D])
                xgT = sb(ctx2, "xgT", [P, KD, P])
                b1 = sb(ctx2, "b1", [P, NE * FF])
                h = sb(ctx2, "h", [P, FF])
                hT = sb(ctx2, "hT", [P, 2, P])
                yo = sb(ctx2, "yo", [P, D])
                per = [sems(ctx2, *(f"{n}{b}" for n in ("xg_in", "xg_T", "xgT_saved", "up_mm", "h_sum", "h_gelu",
                                                        "h_T", "hT_saved", "down_mm", "y_saved", "y_out"))) for b in range(2)]
                b1_in, = sems(ctx2, "b1_in")
                block = ctx2.enter_context(nc.Block())

                def load_b1(sp, b):
                    sp.dma_start(b1[:, :], a[("b1_sp", "b1_fq")[b]].rearrange("e f -> (e f)").unsqueeze(0).to_broadcast(
                        [P, NE * FF])).then_inc(b1_in, 16)

                @block.sync
                def _(sp):
                    load_b1(sp, 0)
                    load_w2(sp, 0, W2)
                    load_w1(sp, 1)
                    for b in range(2):
                        xg_in, xg_T, xgT_saved, up_mm, h_sum, h_gelu, h_T, hT_saved, down_mm, y_saved, y_out = per[b]

                        def load_x(j):
                            after(sp, xg_T, j)
                            sp.dma_start(xg[:, :], routed[b][ds(j * P, P), :]).then_inc(xg_in, 16)

                        def store(j):
                            sp.wait_ge(y_saved, j + 1)
                            sp.dma_start(expert_out[b][ds(j * P, P), :], yo[:, :]).then_inc(y_out, 16)

                        if b == 1:
                            sp.wait_ge(per[0][1], ST)
                            sp.wait_ge(per[0][4], ST)
                            load_b1(sp, 1)
                            sp.wait_ge(per[0][8], ST)
                            load_w2(sp, 1, W2)
                        for j in range(3):
                            load_x(j)
                        with sp.Fori(3, ST) as j:
                            load_x(j)
                            store(j - 3)
                        for j in range(ST - 3, ST):
                            store(j)
                        sp.wait_ge(y_out, 16 * ST)

                @block.tensor
                def _(pe):
                    for b in range(2):
                        xg_in, xg_T, xgT_saved, up_mm, h_sum, h_gelu, h_T, hT_saved, down_mm, y_saved, y_out = per[b]

                        def turn_x(j):
                            pe.wait_ge(xg_in, 16 * (j + 1))
                            after(pe, xgT_saved, j)
                            for k in range(KD):
                                m = pe.transpose(PS[1][:, k * P:(k + 1) * P], xg[:, k * P:(k + 1) * P], ident[:, :])
                            m.then_inc(xg_T, 1)

                        def up(j):
                            e = pe.value_load(tile_expert[0:1, ds(b * ST + j, 1)], min_val=0, max_val=NE - 1)
                            pe.wait_ge(xgT_saved, j + 1)
                            after(pe, h_sum, j)
                            for k in range(KD):
                                m = pe.matmul(PS[0][:, 0:FF], xgT[:, k, :], W1[b][:, ds(e * (KD * FF) + k * FF, FF)],
                                              start=(k == 0), stop=(k == KD - 1))
                            m.then_inc(up_mm, 1)

                        def turn_h(j):
                            pe.wait_ge(h_gelu, j + 1)
                            after(pe, hT_saved, j)
                            for f in range(2):
                                m = pe.transpose(PS[3][:, f * P:(f + 1) * P], h[:, f * P:(f + 1) * P], ident[:, :])
                            m.then_inc(h_T, 1)

                        def down(j):
                            e = pe.value_load(tile_expert[0:1, ds(b * ST + j, 1)], min_val=0, max_val=NE - 1)
                            pe.wait_ge(hT_saved, j + 1)
                            after(pe, y_saved, j)
                            for f in range(2):
                                m = pe.matmul(PS[2][:, :], hT[:, f, :], W2[:, ds(e * (2 * D) + f * D, D)],
                                              start=(f == 0), stop=(f == 1))
                            m.then_inc(down_mm, 1)

                        graph.products(pe, q_bank[b], BANK_Q[b])
                        qt = q_bank[b] + BANK_Q[b] - TILE_Q
                        pe.wait_ge(w1_in, 16 * NE * (b + 1))
                        if b == 1:
                            pe.wait_ge(per[0][9], ST)
                            pe.wait_ge(per[0][7], ST)
                        turn_x(0)
                        up(0)
                        turn_x(1)
                        turn_h(0)
                        pe.wait_ge(w2_in, 16 * NE * (b + 1))
                        with pe.Fori(1, ST - 1) as j:
                            up(j)
                            turn_x(j + 1)
                            graph.multiply(pe, TILE_Q * j + qt, 0)
                            down(j - 1)
                            turn_h(j)
                            graph.multiply(pe, TILE_Q * j + (qt + 1), 1)
                        up(ST - 1)
                        down(ST - 2)
                        turn_h(ST - 1)
                        down(ST - 1)

                @block.vector
                def _(dve):
                    for b in range(2):
                        xg_in, xg_T, xgT_saved, up_mm, h_sum, h_gelu, h_T, hT_saved, down_mm, y_saved, y_out = per[b]

                        def save_x(j):
                            dve.wait_ge(xg_T, j + 1)
                            after(dve, up_mm, j)
                            dve.tensor_copy(xgT[:, :, :].rearrange("p k n -> p (k n)"), PS[1][:, :]).then_inc(xgT_saved, 1)

                        def bias(j):
                            e = dve.value_load(tile_expert[0:1, ds(b * ST + j, 1)], min_val=0, max_val=NE - 1)
                            dve.wait_ge(up_mm, j + 1)
                            after(dve, h_T, j)
                            if b == 1 and isinstance(j, int) and j == 0:
                                dve.wait_ge(per[0][6], ST)
                            dve.tensor_tensor(h[:, :], PS[0][:, 0:FF], b1[:, ds(e * FF, FF)], ALU.add).then_inc(h_sum, 1)
                        graph.sums(dve, q_bank[b], BANK_Q[b])
                        qt = q_bank[b] + BANK_Q[b] - TILE_Q
                        dve.wait_ge(b1_in, 16 * (b + 1))
                        save_x(0)
                        bias(0)
                        save_x(1)
                        with dve.Fori(1, ST - 2) as j:
                            bias(j)
                            save_x(j + 1)
                            graph.sums(dve, TILE_Q * j + qt, TILE_Q)
                        bias(ST - 2)
                        save_x(ST - 1)
                        graph.sums(dve, TILE_Q * (ST - 2) + qt, TILE_Q, last=b == 1)
                        bias(ST - 1)

                @block.scalar
                def _(act):
                    for b in range(2):
                        xg_in, xg_T, xgT_saved, up_mm, h_sum, h_gelu, h_T, hT_saved, down_mm, y_saved, y_out = per[b]

                        def gelu(j):
                            act.wait_ge(h_sum, j + 1)
                            act.activation(h[:, :], h[:, :], ACT.Gelu).then_inc(h_gelu, 1)

                        def save_h(j):
                            act.wait_ge(h_T, j + 1)
                            after(act, down_mm, j)
                            act.copy(hT[:, :, :].rearrange("p f n -> p (f n)"), PS[3][:, 0:FF]).then_inc(hT_saved, 1)

                        def save_y(j):
                            act.wait_ge(down_mm, j + 1)
                            after(act, y_out, 16 * j)
                            act.copy(yo[:, :], PS[2][:, :]).then_inc(y_saved, 1)
                        if b == 1:
                            act.wait_ge(per[0][10], 16 * ST)
                        gelu(0)
                        save_h(0)
                        with act.Fori(1, ST) as j:
                            gelu(j)
                            save_y(j - 1)
                            save_h(j)
                        save_y(ST - 1)

            with ExitStack() as ctx2:
                back = sb(ctx2, "back", [P, 2, NT, D])
                got = sems(ctx2, *(f"got{t}" for t in range(NT)))
                bias_mm, added, step = sems(ctx2, "bias_mm", "expert_added", "combine_step")
                block = ctx2.enter_context(nc.Block())

                def rows(t):
                    return P if t < NT - 1 else LAST

                @block.gpsimd
                def _(pool):
                    for t in range(NT):
                        n = rows(t)
                        for b in range(2):
                            pool.indirect_dma_start(
                                back[0:n, b, t, :], None, expert_out[b],
                                bass.IndirectOffsetOnAxis(ap=slot[0:n, 2 * t + b:2 * t + b + 1], axis=0)).then_inc(got[t], 16)

                @block.tensor
                def _(pe):
                    pe.wait_ge(bias2_in, 16)
                    for t in range(NT):
                        after(pe, step, 3 * (t - 2) + 1)
                        pe.matmul(PS[t % 2][:, :], gated_hot[0:2 * NE + 1, t * P:(t + 1) * P], bias2[:, :],
                                  start=True, stop=True).then_inc(bias_mm, 1)

                @block.vector
                def _(dve):
                    ch = Chain(dve, step)
                    for t in range(NT):
                        n = rows(t)
                        dve.wait_ge(bias_mm, t + 1)
                        ch.mark(dve.tensor_tensor(X[:, t, :], X[:, t, :], PS[t % 2][:, :], ALU.add))
                        dve.wait_ge(got[t], 32)
                        for b in range(2):
                            ch.wait()
                            ch.mark(dve.scalar_tensor_tensor(out=X[0:n, t, :], in0=back[0:n, b, t, :],
                                                             scalar=gate[0:n, 2 * t + b:2 * t + b + 1], in1=X[0:n, t, :],
                                                             op0=ALU.mult, op1=ALU.add))

        with ExitStack() as g3:
            AT = sb(g3, "AT", [P, NT, NP])
            M = sb(g3, "M", [P, NT, FF])
            valid = sb(g3, "valid", [P, NT])
            wm = sb(g3, "wm", [P, KD, FF])
            w1 = sb(g3, "l1_w1", [P, KD, P])
            w2 = sb(g3, "l1_w2", [P, D])
            rows3 = sb(g3, "rows3", [P, NROW])
            w3_in, = sems(g3, "block3_w_in")

            def bias_row(name):
                at, n = BIAS_ROWS[name]
                return rows3[:, at:at + n]

            general_passes("_a", A, True)

            with ExitStack() as ctx:
                total = sb(ctx, "total", [P, NT])
                inv = sb(ctx, "inv", [P, NT])
                strip = sb(ctx, "strip", [P, 2, NT, P])
                sums, step, normed, strips, turned, saved = sems(
                    ctx, "row_sums", "inv_step", "a_normed", "strips", "a_turned", "at_saved")
                block = ctx.enter_context(nc.Block())

                @block.sync
                def _(sp):
                    sp.dma_start(wm[:, :, :], a["wm"].rearrange("(k p) f -> p k f", p=P)).then_inc(w3_in, 16)
                    sp.dma_start(w1[:, :, :], a["l1_w1"].rearrange("(k p) f -> p k f", p=P)).then_inc(w3_in, 16)
                    sp.dma_start(w2[:, :], a["l1_w2"]).then_inc(w3_in, 16)
                    sp.dma_start(rows3[:, :], a["bias_rows"].to_broadcast([P, NROW])).then_inc(w3_in, 16)

                @block.vector
                def _(dve):
                    ch = Chain(dve, step)
                    for s in range(NT):
                        dve.tensor_reduce(total[:, s:s + 1], A[:, s, :], AX.X, ALU.add).then_inc(sums, 1)
                    dve.wait_ge(sums, NT)
                    ch.mark(dve.tensor_scalar(inv[:, :], total[:, :], 1e-6, None, ALU.add))
                    ch.mark(dve.tensor_scalar(valid[:, :], total[:, :], 0.0, None, ALU.is_gt))
                    ch.wait()
                    ch.mark(dve.reciprocal(inv[:, :], inv[:, :]))
                    ch.wait()
                    for s in range(NT):
                        dve.tensor_scalar(A[:, s, :], A[:, s, :], inv[:, s:s + 1], None, ALU.mult).then_inc(normed, 1)

                    def save(i):
                        for p in range(2):
                            d = 2 * i + p
                            dve.wait_ge(turned, 3 * d + 1)
                            dve.tensor_copy(AT[:, ds(d, 1), 0:4 * P].rearrange("p a n -> p (a n)"), PS[4 * p][:, :]).then_inc(saved, 1)
                            dve.wait_ge(turned, 3 * d + 3)
                            dve.tensor_copy(AT[:, ds(d, 1), 8 * P:NP].rearrange("p a n -> p (a n)"),
                                            PS[4 * p + 2][:, 0:2 * P]).then_inc(saved, 1)
                    looped(dve, NT // 2, save)

                act_saved, = sems(ctx, "at_saved_act")

                @block.scalar
                def _(act):
                    def pair(i):
                        for p in range(2):
                            d = 2 * i + p
                            act.wait_ge(normed, NT)
                            after(act, turned, 3 * (d - 2) + 3 if isinstance(i, int) else 3 * d - 3)
                            act.copy(strip[:, p, :, :], A[:, :, ds(d * P, P)]).then_inc(strips, 1)
                            if p == 0:
                                if isinstance(i, int):
                                    continue
                            act.wait_ge(turned, 3 * (d - 1) + 2 if isinstance(i, int) else 3 * d - 1)
                            act.copy(AT[:, ds(d - 1, 1), 4 * P:8 * P].rearrange("p a n -> p (a n)"),
                                     PS[4 * (1 - p) + 1][:, :]).then_inc(act_saved, 1)
                    looped(act, NT // 2, pair)
                    act.wait_ge(turned, 3 * NT - 1)
                    act.copy(AT[:, NT - 1, 4 * P:8 * P], PS[5][:, :]).then_inc(act_saved, 1)

                @block.tensor
                def _(pe):
                    def pair(i):
                        for p in range(2):
                            d = 2 * i + p
                            pe.wait_ge(strips, d + 1)
                            after(pe, saved, 2 * (d - 2) + 2 if isinstance(i, int) else 2 * d - 2)
                            after(pe, act_saved, d - 1)
                            for s in range(NT):
                                m = pe.transpose(PS[4 * p + s // 4][:, (s % 4) * P:(s % 4 + 1) * P], strip[:, p, s, :], ident[:, :])
                                if s in (3, 7, 9):
                                    m.then_inc(turned, 1)
                    looped(pe, NT // 2, pair)
            norm_phase("3", proj=(wm, bias_row("bm"), M), weights_in=(w3_in, 64))

            with ExitStack() as ctx:
                msg = sb(ctx, "msg", [P, KD, CH])
                h1 = sb(ctx, "h1", [P, CH])
                hn = sb(ctx, "hn", [P, TPC, P])
                hnT = sb(ctx, "hnT", [P, CH])
                y3 = sb(ctx, "y3", [P, TPC, D])
                st3 = sb(ctx, "st3", [P, TPC, 6])
                mv3 = sb(ctx, "mv3", [P, TPC, 2])
                idle = sb(ctx, "idle", [P, 1])
                sd3 = sb(ctx, "sd3", [P, TPC])
                agg_mm, msg_saved, h1_mm, h1_saved, h1_T, stat3, root3, hn_ready, hn_T, hnT_saved, out_mm, out_step = sems(
                    ctx, "att_mm", "msg_saved", "h1_mm", "h1_saved", "h1_T", "stat3", "root3", "hn_ready", "hn_T", "hnT_saved",
                    "out_mm3", "out_step3")
                block = ctx.enter_context(nc.Block())
                LNS, OUTS = 11, 6

                def aggregate(pe, c, f):
                    after(pe, msg_saved, KD * c + f - 1)
                    for s in range(NT):
                        if f < 2:
                            lhs, rhs = M[:, s, f * P:(f + 1) * P], AT[:, s, ds(c * CH, CH)]
                        else:
                            lhs, rhs = M[:, s, (f - 2) * P:(f - 1) * P], A[:, s, ds(c * CH, CH)]
                        m = pe.matmul(PS[f % 2][:, 0:CH], lhs, rhs, start=(s == 0), stop=(s == NT - 1))
                    m.then_inc(agg_mm, 1)

                def dense1(pe, c):
                    pe.wait_ge(msg_saved, KD * c + KD)
                    after(pe, h1_saved, c)
                    for k in range(KD):
                        m = pe.matmul(PS[2][:, 0:CH], w1[:, k, :], msg[:, k, :], start=(k == 0), stop=(k == KD - 1))
                    m.then_inc(h1_mm, 1)

                def turn_h1(pe, c):
                    pe.wait_ge(h1_saved, c + 1)
                    after(pe, hn_ready, c)
                    for j in range(TPC):
                        m = pe.transpose(PS[3][:, j * P:(j + 1) * P], h1[:, j * P:(j + 1) * P], ident[:, :])
                    m.then_inc(h1_T, 1)

                def turn_hn(pe, c):
                    pe.wait_ge(hn_ready, c + 1)
                    after(pe, hnT_saved, c)
                    for j in range(TPC):
                        m = pe.transpose(PS[4][:, j * P:(j + 1) * P], hn[:, j, :], ident[:, :])
                    m.then_inc(hn_T, 1)

                def dense2(pe, c):
                    pe.wait_ge(hnT_saved, c + 1)
                    after(pe, out_step, OUTS * c)
                    for j in range(TPC):
                        m = pe.matmul(PS[5 + j][:, :], hnT[:, j * P:(j + 1) * P], w2[:, :], start=True, stop=True)
                    m.then_inc(out_mm, 1)

                @block.tensor
                def _(pe):
                    for f in range(KD):
                        aggregate(pe, 0, f)
                    dense1(pe, 0)

                    def chunk(c, before):
                        aggregate(pe, c, 0)
                        turn_h1(pe, before)
                        aggregate(pe, c, 1)
                        turn_hn(pe, before)
                        aggregate(pe, c, 2)
                        dense2(pe, before)
                        aggregate(pe, c, 3)
                        dense1(pe, c)
                    chunk(1, 0)
                    with pe.Fori(2, NC) as c:
                        chunk(c, c - 1)
                    turn_h1(pe, NC - 1)
                    turn_hn(pe, NC - 1)
                    dense2(pe, NC - 1)

                @block.scalar
                def _(act):
                    def save(c, f):
                        act.wait_ge(agg_mm, KD * c + f + 1)
                        after(act, h1_mm, c)
                        act.copy(msg[:, f, :], PS[f % 2][:, 0:CH]).then_inc(msg_saved, 1)

                    def save_h1(c):
                        act.wait_ge(h1_mm, c + 1)
                        after(act, h1_T, c)
                        act.activation(h1[:, :], PS[2][:, 0:CH], ACT.Identity,
                                       bias=bcol[:, BIAS_COLS["l1_b1"]:BIAS_COLS["l1_b1"] + 1]).then_inc(h1_saved, 1)

                    def root(c):
                        act.wait_ge(stat3, LNS * c + 2 * TPC)
                        act.activation(sd3[:, :], mv3[:, :, 1], ACT.Sqrt, bias=eps[:, 0:1]).then_inc(root3, 1)

                    def save_hn(c):
                        act.wait_ge(hn_T, c + 1)
                        after(act, out_mm, c)
                        act.copy(hnT[:, :], PS[4][:, 0:CH]).then_inc(hnT_saved, 1)

                    for f in range(KD):
                        save(0, f)
                    save_h1(0)

                    def chunk(c, before):
                        save(c, 0)
                        root(before)
                        save(c, 1)
                        save_hn(before)
                        save(c, 2)
                        save(c, 3)
                        save_h1(c)
                    chunk(1, 0)
                    with act.Fori(2, NC) as c:
                        chunk(c, c - 1)
                    root(NC - 1)
                    save_hn(NC - 1)

                @block.vector
                def _(dve):
                    def norm(c):
                        ch = Chain(dve, stat3)
                        ch.at(LNS * c)
                        dve.wait_ge(h1_T, c + 1)
                        after(dve, hn_T, c)
                        for j in range(TPC):
                            ch.mark(dve.bn_stats(st3[:, j, :], PS[3][:, j * P:(j + 1) * P]))
                        ch.wait()
                        dve.memset(idle[:, :], 0.0)
                        ch.mark(dve.bn_aggr(mv3[:, 0, :], st3[:, 0, :]))
                        ch.mark(dve.bn_aggr(mv3[:, 1, :], st3[:, 1, :]))
                        dve.wait_ge(root3, c + 1)
                        ch.mark(dve.reciprocal(sd3[:, :], sd3[:, :]))
                        ch.wait()
                        for j in range(TPC):
                            ch.mark(dve.tensor_scalar(hn[:, j, :], PS[3][:, j * P:(j + 1) * P], mv3[:, j, 0:1], sd3[:, j:j + 1],
                                                      ALU.subtract, ALU.mult))
                        ch.wait()
                        for j in range(TPC):
                            ch.mark(dve.tensor_tensor(hn[:, j, :], hn[:, j, :], bias_row("gamma"), ALU.mult))
                        ch.wait()
                        for j in range(TPC):
                            ch.mark(dve.tensor_tensor(hn[:, j, :], hn[:, j, :], bias_row("beta"), ALU.add))
                        ch.wait()
                        assert ch.n == LNS
                        dve.tensor_scalar(hn[:, :, :], hn[:, :, :], 0.0, None, ALU.max).then_inc(hn_ready, 1)

                    def add(c):
                        ch = Chain(dve, out_step)
                        ch.at(OUTS * c)
                        dve.wait_ge(out_mm, c + 1)
                        for j in range(TPC):
                            ch.mark(dve.tensor_tensor(y3[:, j, :], PS[5 + j][:, :], bias_row("l1_b2"), ALU.add))
                        ch.wait()
                        for j in range(TPC):
                            ch.mark(dve.tensor_scalar(y3[:, j, :], y3[:, j, :], 0.0, valid[:, ds(TPC * c + j, 1)], ALU.max, ALU.mult))
                        ch.wait()
                        for j in range(TPC):
                            x_t = tile_of(X, TPC * c + j)
                            ch.mark(dve.tensor_tensor(x_t, x_t, y3[:, j, :], ALU.add))
                        assert ch.n == OUTS
                    norm(0)
                    add(0)
                    with dve.Fori(1, NC) as c:
                        norm(c)
                        add(c)

        with ExitStack() as g4:
            XT = sb(g4, "XT4", [P, KD, NP])
            wt = [sb(g4, f"mix_w{i}", [P, KD, D]) for i in range(2)]
            rows4 = sb(g4, "rows4", [P, D])
            w4_in, masked = sems(g4, "mix_w_in", "masked")

            def load(sp):
                for i in range(2):
                    sp.dma_start(wt[i][:, :, :], a[f"mix_w{i + 1}"].rearrange("(k p) s -> p k s", p=P)).then_inc(w4_in, 16)
                at, n = BIAS_ROWS["ffn_b2"]
                sp.dma_start(rows4[:, :], a["bias_rows"][:, at:at + n].to_broadcast([P, D])).then_inc(w4_in, 16)
            norm_phase("4", XT=XT, sync=load)
            H = sb(g4, "H4", [P, KD, CH])
            up_mm, h_saved, down_mm, out_added, x_out = sems(g4, "mix_up_mm", "mix_h", "mix_down_mm", "mix_added", "x_out")
            block = g4.enter_context(nc.Block())

            @block.gpsimd
            def _(pool):
                pool.wait_ge(w4_in, 48)
                for i in range(2):
                    for k in range(KD):
                        w = wt[i][:, k, k * P:(k + 1) * P]
                        pool.affine_select(out=w, in_=w, compare_op=ALU.is_ge, fill=0.0, base=0, pattern=[[1, P]],
                                           channel_multiplier=-1).then_inc(masked, 1)

            @block.tensor
            def _(pe):
                pe.wait_ge(masked, 2 * KD)

                def chunk(c):
                    for s in range(KD):
                        after(pe, h_saved, KD * c + s - 1)
                        for k in range(s + 1):
                            m = pe.matmul(PS[s % 2][:, 0:CH], wt[0][:, k, s * P:(s + 1) * P], XT[:, k, ds(c * CH, CH)],
                                          start=(k == 0), stop=(k == s))
                        m.then_inc(up_mm, 1)
                    pe.wait_ge(h_saved, KD * c + KD)
                    for j in range(TPC):
                        after(pe, out_added, 2 * TPC * c)
                        for k in range(KD):
                            m = pe.matmul(PS[2 + j][:, k * P:D], H[:, k, j * P:(j + 1) * P], wt[1][:, k, k * P:D],
                                          start=(k == 0), stop=(k == KD - 1), skip_group_check=True)
                        m.then_inc(down_mm, 1)
                looped(pe, NC, chunk)

            @block.scalar
            def _(act):
                def chunk(c):
                    for s in range(KD):
                        act.wait_ge(up_mm, KD * c + s + 1)
                        after(act, down_mm, TPC * c)
                        col = BIAS_COLS["ffn_b1"] + s
                        act.activation(H[:, s, :], PS[s % 2][:, 0:CH], ACT.Gelu, bias=bcol[:, col:col + 1]).then_inc(h_saved, 1)
                looped(act, NC, chunk)

            @block.vector
            def _(dve):
                def chunk(c):
                    for j in range(TPC):
                        x_t = tile_of(X, TPC * c + j)
                        dve.wait_ge(down_mm, TPC * c + j + 1)
                        dve.tensor_tensor(x_t, x_t, PS[2 + j][:, :], ALU.add).then_inc(out_added, 1)
                        dve.wait_ge(out_added, 2 * TPC * c + 2 * j + 1)
                        dve.tensor_tensor(x_t, x_t, rows4[:, :], ALU.add).then_inc(out_added, 1)
                looped(dve, NC, chunk)

            @block.sync
            def _(sp):
                last = TPC * (NC - 1)
                with sp.Fori(0, NC - 1) as c:
                    sp.wait_ge(out_added, 2 * TPC * c + 2 * TPC)
                    sp.dma_start(out[ds(c * CH, CH), :].rearrange("(t p) d -> p t d", p=P), X[:, ds(TPC * c, TPC), :]).then_inc(x_out, 16)
                sp.wait_ge(out_added, 2 * NT)
                sp.dma_start(out[last * P:(NT - 1) * P, :], X[:, last, :]).then_inc(x_out, 16)
                sp.dma_start(out[(NT - 1) * P:N, :], X[0:LAST, NT - 1, :]).then_inc(x_out, 16)
                sp.wait_ge(x_out, 16 * (NC + 1))


_COLS = [("gnn_b1", "L0_gnn_b1"), ("gnn_br1", "L0_gnn_br1"), ("gnn_b2", "L0_gnn_b2"), ("gnn_br2", "L0_gnn_br2"),
         ("bs1", "L0_ffn_bs1"), ("l1_b1", "L1_gnn_b1"), ("ffn_b1", "L1_ffn_b1")]
_ROWS = [("bm", "L1_gnn_bm"), ("gamma", "L1_gnn_gamma"), ("beta", "L1_gnn_beta"),
         ("l1_b2", "L1_gnn_b2"), ("ffn_b2", "L1_ffn_b2")]


def _laid_out(inputs):
    import numpy as np
    g = {k: np.asarray(v) for k, v in inputs.items()}
    a = {k: g[k] for k in ("x", "src", "dst", "edge_weight")}
    a["bias_cols"] = np.ascontiguousarray(np.concatenate([g[n].reshape(-1, P).T for _, n in _COLS], axis=1))
    a["bias_rows"] = np.concatenate([g[n] for _, n in _ROWS]).reshape(1, -1)
    for l in "12":
        a["gnn_w" + l] = np.ascontiguousarray(g["L0_gnn_W" + l].T)
        a["gate_w" + l] = np.ascontiguousarray(g["L0_gnn_Wr" + l].T)
    a["router_w"] = np.ascontiguousarray(np.concatenate([g["L0_ffn_Wr_sp"], g["L0_ffn_Wr_fq"]], axis=1))
    a["router_b"] = np.concatenate([g["L0_ffn_br_sp"], g["L0_ffn_br_fq"]]).reshape(-1, 1)
    a["ws1"], a["ws2"] = g["L0_ffn_Ws1"], g["L0_ffn_Ws2"]
    for b in ("sp", "fq"):
        for n in ("W1", "b1", "W2"):
            a[f"{n}_{b}"] = g[f"L0_ffn_{n}_{b}"]
    a["b2_all"] = np.concatenate([g["L0_ffn_b2_sp"], g["L0_ffn_b2_fq"], g["L0_ffn_bs2"].reshape(1, -1)], axis=0)
    a["wm"], a["l1_w1"], a["l1_w2"] = g["L1_gnn_Wm"], g["L1_gnn_W1"], g["L1_gnn_W2"]
    a["mix_w1"] = np.ascontiguousarray(g["L1_ffn_W1"].T)
    a["mix_w2"] = np.ascontiguousarray(g["L1_ffn_W2"].T)
    return a


def _program(nc, arrays):
    aps = {k: nc.dram_tensor(f"in_{k}", v.shape, mybir.dt.from_np(v.dtype), kind="ExternalInput").ap()
           for k, v in arrays.items()}
    out = nc.dram_tensor("out_x", (N, D), F32, kind="ExternalOutput").ap()
    routed = [nc.dram_tensor(f"routed{b}", (SLOTS, D), F32, kind="Internal").ap() for b in range(2)]
    expert_out = [nc.dram_tensor(f"expert_out{b}", (SLOTS, D), F32, kind="Internal").ap() for b in range(2)]
    build(nc, aps, out, routed, expert_out)


def kernel(**inputs):
    import concourse.bacc as bacc
    from concourse.bass_utils import run_bass_kernel_spmd
    arrays = _laid_out(inputs)
    nc = bacc.Bacc("TRN2", target_bir_lowering=False, num_devices=1)
    _program(nc, arrays)
    r = run_bass_kernel_spmd(nc, [{f"in_{k}": v for k, v in arrays.items()}], core_ids=[0])
    return r.results[0]["out_x"]
```

```python
from contextlib import ExitStack

import concourse.bass as bass
import concourse.mybir as mybir
from concourse.alu_op_type import AluOpType as ALU

F32 = mybir.dt.float32
BF16 = mybir.dt.bfloat16
I32 = mybir.dt.int32
ACT = mybir.ActivationFunctionType
AX = mybir.AxisListType
ds = bass.ds

P = 128
N = 1250
NT = -(-N // P)
NP = NT * P
LAST = N - (NT - 1) * P
D = 512
KD = D // P
CH = 256
NC = NP // CH
TPC = CH // P
E = 41250
SUB = 3
CE = SUB * P
Q = -(-E // CE)
W = 16
KW = NT * W
CW = NP + W
PASSES = -(-NP // W)
FF = 256
NE = 8
ST = (N - NE) // P + NE
SLOTS = ST * P
EPS = 1e-5
LOADS = 4
FAR = 4096.0

BIAS_COLS = {}
_at = 0
for _name, _n in (("gnn_b1", 4), ("gnn_br1", 4), ("gnn_b2", 4), ("gnn_br2", 4), ("bs1", 2),
                  ("l1_b1", 1), ("ffn_b1", 4), ("bm", 2)):
    BIAS_COLS[_name] = _at
    _at += _n
NBIAS = _at
BIAS_ROWS = {}
_at = 0
for _name, _n in (("gamma", P), ("beta", P), ("l1_b2", D), ("ffn_b2", D)):
    BIAS_ROWS[_name] = (_at, _n)
    _at += _n
NROW = _at


class Chain:

    def __init__(self, eng, sem):
        self.eng, self.sem, self.base, self.n = eng, sem, 0, 0

    def at(self, base):
        self.base, self.n = base, 0

    def mark(self, ins):
        ins.then_inc(self.sem, 1)
        self.n += 1
        return self.base + self.n

    def wait(self, back=0):
        self.eng.wait_ge(self.sem, self.base + self.n - back)


def after(eng, sem, value):
    if not isinstance(value, int) or value > 0:
        eng.wait_ge(sem, value)


def looped(eng, count, body):
    body(0)
    with eng.Fori(1, count) as i:
        body(i)


def build(nc, a, out, routed, expert_out):
    with ExitStack() as top:
        def sb(ctx, name, shape, dt=F32):
            return ctx.enter_context(nc.sbuf_tensor(name, shape, dt))

        def sems(ctx, *names):
            return [ctx.enter_context(nc.semaphore(n)) for n in names]

        cleared_slots, = sems(top, "cleared_slots")
        first_reused = cleared_slots.num + 1

        PS = [top.enter_context(nc.psum_tensor(f"PS{i}", [P, 512], F32)) for i in range(8)]

        X = sb(top, "X", [P, NT, D])
        ident = sb(top, "ident", [P, P])
        ones = sb(top, "ones", [P, P])
        iota = sb(top, "iota", [P, KW, SUB], BF16)
        bcol = sb(top, "bcol", [P, NBIAS])
        eps = sb(top, "eps", [P, 1])
        stats = sb(top, "stats", [P, NT, 6])
        mv = sb(top, "mv", [P, NT, 2])
        std = sb(top, "std", [P, NT])
        rstd = sb(top, "rstd", [P, NT])
        key = sb(top, "key", [P, Q, SUB], BF16)
        srow = sb(top, "srow", [P, Q, SUB], BF16)
        part = sb(top, "part", [P, Q, 3, SUB], BF16)
        first = sb(top, "first", [1, Q])
        base_row = sb(top, "base_row", [1, Q], I32)
        flag = sb(top, "flag", [1, 1], I32)
        rel = sb(top, "rel", [Q, CE])
        sbw = sb(top, "sbw", [Q, CE])

        scope1 = top.enter_context(ExitStack())
        wexp = sb(scope1, "wexp", [P, Q, SUB])
        C = sb(scope1, "C", [P, NT, CW])
        cleared, = sems(scope1, "cleared_c")

        def tile_of(t3, t):
            return t3[:, ds(t, 1), :].rearrange("p a d -> p (a d)")

        with ExitStack() as ctx:
            s32 = sb(ctx, "s32", [Q, CE], I32)
            d32 = sb(ctx, "d32", [Q, CE], I32)
            wrow = sb(ctx, "wrow", [Q, CE])
            lo32 = sb(ctx, "lo32", [Q, CE], I32)
            hi32 = sb(ctx, "hi32", [Q, CE], I32)
            srowr = sb(ctx, "srowr", [Q, CE])
            past = sb(ctx, "past", [Q, CE])
            keyr = sb(ctx, "keyr", [Q, CE])
            est = sb(ctx, "est", [Q, 4])
            fl = sb(ctx, "fl", [1, 4])
            negmax = sb(ctx, "negmax", [P, 1])
            edges_in, consts_in, x_in = sems(ctx, "edges_in", "consts_in", "x_in")
            pads, consts, ident_zero = sems(ctx, "pads", "consts", "ident_zero")
            step, spans, keys = sems(ctx, "prep_step", "spans", "keys")
            spans_T, tables_T, tables, wmax, wmax_all, weights = sems(
                ctx, "spans_T", "tables_T", "tables_done", "wmax", "wmax_all", "weights")
            block = ctx.enter_context(nc.Block())

            @block.sync
            def _(sp):
                full, rest = Q - 1, E - (Q - 1) * CE
                sp.wait_ge(pads, 4)
                for t, e in ((s32, a["src"]), (d32, a["dst"]), (wrow, a["edge_weight"])):
                    sp.dma_start(t[0:full, :], e[0:full * CE].rearrange("(q e) -> q e", e=CE)).then_inc(edges_in, 16)
                    sp.dma_start(t[full:Q, 0:rest], e[full * CE:E].rearrange("(q e) -> q e", q=1)).then_inc(edges_in, 16)
                sp.dma_start(X[:, 0:NT - 1, :], a["x"][0:(NT - 1) * P, :].rearrange("(t p) d -> p t d", p=P)).then_inc(x_in, 16)
                sp.dma_start(X[0:LAST, NT - 1, :], a["x"][(NT - 1) * P:N, :]).then_inc(x_in, 16)
                sp.dma_start(bcol[:, :], a["bias_cols"]).then_inc(consts_in, 16)
                sp.wait_ge(x_in, 32)
                sp.wait_ge(consts_in, 16)

            @block.gpsimd
            def _(pool):
                pool.memset(s32[:, :], 4 * NP).then_inc(pads, 1)
                pool.memset(d32[:, :], N - 1).then_inc(pads, 1)
                pool.memset(wrow[:, :], 0.0).then_inc(pads, 1)
                pool.memset(X[:, NT - 1, :], 0.0).then_inc(pads, 1)
                pool.memset(ident[:, :], 0.0).then_inc(ident_zero, 1)
                pool.memset(ones[:, :], 1.0).then_inc(consts, 1)
                pool.memset(eps[:, :], EPS).then_inc(consts, 1)
                pool.iota(iota[:, :, :], pattern=[[1, KW], [0, SUB]], base=0, channel_multiplier=0,
                          allow_small_or_imprecise_dtypes=True).then_inc(consts, 1)
                pool.wait_ge(ident_zero, 1)
                pool.affine_select(out=ident[:, :], in_=ident[:, :], compare_op=ALU.not_equal, fill=1.0, base=0,
                                   pattern=[[-1, P]], channel_multiplier=1).then_inc(consts, 1)
                pool.memset(C[:, :, :], 0.0).then_inc(cleared, 1)

            @block.vector
            def _(dve):
                ch = Chain(dve, step)
                dve.wait_ge(edges_in, 96)
                ch.mark(dve.tensor_scalar(lo32[:, :], s32[:, :], P - 1, None, ALU.bitwise_and))
                ch.mark(dve.tensor_scalar(hi32[:, :], s32[:, :], 7, None, ALU.arith_shift_right))
                ch.mark(dve.tensor_copy(rel[:, :], d32[:, :]))
                ch.wait()
                ch.mark(dve.tensor_scalar(sbw[:, :], hi32[:, :], float(W), None, ALU.mult))
                ch.mark(dve.tensor_reduce(est[:, 0:1], rel[:, :], AX.X, ALU.min))
                ch.mark(dve.tensor_reduce(est[:, 3:4], rel[:, :], AX.X, ALU.max))
                ch.mark(dve.tensor_reduce(est[:, 2:3], wrow[:, :], AX.X, ALU.max))
                ch.wait()
                dve.tensor_tensor(est[:, 1:2], est[:, 3:4], est[:, 0:1], ALU.subtract).then_inc(spans, 1)
                ch.mark(dve.tensor_scalar(rel[:, :], rel[:, :], est[:, 0:1], None, ALU.subtract))
                ch.wait()
                ch.mark(dve.tensor_scalar(past[:, :], rel[:, :], float(W), FAR, ALU.is_ge, ALU.mult))
                ch.mark(dve.tensor_tensor(keyr[:, :], sbw[:, :], rel[:, :], ALU.add))
                ch.wait()
                dve.tensor_copy(srowr[:, :], lo32[:, :]).then_inc(keys, 1)
                dve.tensor_tensor(keyr[:, :], keyr[:, :], past[:, :], ALU.add).then_inc(keys, 1)
                dve.wait_ge(spans_T, 3)
                ch.mark(dve.tensor_copy(first[:, :], PS[0][0:1, 0:Q]))
                ch.mark(dve.tensor_reduce(fl[:, 0:1], PS[0][0:1, 128:128 + Q], AX.X, ALU.max))
                ch.mark(dve.tensor_reduce(fl[:, 1:2], PS[0][0:1, 256:256 + Q], AX.X, ALU.max))
                ch.wait()
                ch.mark(dve.tensor_copy(base_row[:, :], first[:, :]))
                ch.mark(dve.tensor_scalar(flag[:, 0:1], fl[:, 0:1], float(W), None, ALU.is_ge))
                dve.tensor_scalar(fl[:, 2:3], fl[:, 1:2], 0.0, -1.0, ALU.max, ALU.mult).then_inc(wmax, 1)
                for i, tab in enumerate((srow, key, wexp)):
                    dve.wait_ge(tables_T, i + 1)
                    dve.tensor_copy(tab[:, :, :], PS[1 + i][:, 0:SUB * Q].rearrange("p (j q) -> p q j", j=SUB)).then_inc(tables, 1)

            @block.tensor
            def _(pe):
                pe.wait_ge(consts, 4)
                pe.wait_ge(spans, 1)
                for i in range(3):
                    pe.transpose(PS[0][0:1, 128 * i:128 * i + Q], est[:, i:i + 1], ident[0:Q, 0:Q]).then_inc(spans_T, 1)
                pe.wait_ge(keys, 2)
                for i, tab in enumerate((srowr, keyr, wrow)):
                    for j in range(SUB):
                        tr = pe.transpose(PS[1 + i][:, j * Q:(j + 1) * Q], tab[:, j * P:(j + 1) * P], ident[0:Q, 0:Q])
                    tr.then_inc(tables_T, 1)
                pe.wait_ge(wmax, 1)
                pe.matmul(PS[4][:, 0:1], ones[0:1, :], fl[:, 2:3], start=True, stop=True).then_inc(wmax_all, 1)

            @block.scalar
            def _(act):
                act.wait_ge(wmax_all, 1)
                act.copy(negmax[:, :], PS[4][:, 0:1]).then_inc(weights, 1)
                act.wait_ge(weights, 1)
                act.wait_ge(tables, 3)
                act.activation(wexp[:, :, :], wexp[:, :, :], ACT.Exp, bias=negmax[:, 0:1]).then_inc(weights, 1)

        def one_hot(dve, to, index, n):
            return dve.tensor_tensor(to, iota[:, 0:n, :], index.to_broadcast([P, n, SUB]), ALU.is_equal)

        def weigh(dve, to, hot, q):
            return dve.tensor_tensor(to, hot.unsqueeze(1).to_broadcast([P, 3, P, SUB]),
                                     part[:, ds(q, 1), :, :].rearrange("p a m j -> p (a m) j").unsqueeze(2).to_broadcast(
                                         [P, 3, P, SUB]), ALU.mult)

        def edge_product(pe, bank, rows, keys):
            n = rows.shape[1]
            for j in range(SUB):
                for m in range(n):
                    mm = pe.matmul(bank[:, 0:KW], rows[:, m, :, j], keys[:, :, j],
                                   start=(j == 0 and m == 0), stop=(j == SUB - 1 and m == n - 1))
            return mm

        def norm_phase(tag, Xn=None, XT=None, sync=None, have_stats=False, pool=None):
            with ExitStack() as ctx:
                RING = 4
                staged = sb(ctx, "staged" + tag, [P, RING, D]) if Xn is None else None
                stat, root, inv, normed, xposed, saved = sems(
                    ctx, *(n + tag for n in ("stat", "root", "inv", "normed", "xposed", "turned")))
                block = ctx.enter_context(nc.Block())
                if sync is not None:
                    block.sync(sync)
                if pool is not None:
                    block.gpsimd(pool)

                def normed_tile(t):
                    return staged[:, t % RING, :] if Xn is None else Xn[:, t, :]

                @block.vector
                def _(dve):
                    if not have_stats:
                        for t in range(NT):
                            dve.bn_stats(stats[:, t, :], X[:, t, :]).then_inc(stat, 1)
                    for t in range(NT):
                        if not have_stats:
                            dve.wait_ge(stat, t + 1)
                        dve.bn_aggr(mv[:, t, :], stats[:, t, :]).then_inc(stat, 1)
                    dve.wait_ge(root, 1)
                    dve.reciprocal(rstd[:, :], std[:, :]).then_inc(inv, 1)
                    dve.wait_ge(inv, 1)
                    for t in range(NT):
                        if Xn is None:
                            after(dve, xposed, t - RING + 1)
                        dve.tensor_scalar(normed_tile(t), X[:, t, :], mv[:, t, 0:1], rstd[:, t:t + 1],
                                          ALU.subtract, ALU.mult).then_inc(normed, 1)

                @block.scalar
                def _(act):
                    act.wait_ge(stat, NT if have_stats else 2 * NT)
                    act.activation(std[:, :], mv[:, :, 1], ACT.Sqrt, bias=eps[:, 0:1]).then_inc(root, 1)
                    for t in range(NT):
                        act.wait_ge(xposed, t + 1)
                        src = PS[t % RING][:, :].rearrange("p (k n) -> p k n", k=KD)
                        act.copy(XT[:, :, t * P:(t + 1) * P], src).then_inc(saved, 1)

                @block.tensor
                def _(pe):
                    for t in range(NT):
                        pe.wait_ge(normed, t + 1)
                        after(pe, saved, t - RING + 1)
                        for k in range(KD):
                            tr = pe.transpose(PS[t % RING][:, k * P:(k + 1) * P], normed_tile(t)[:, k * P:(k + 1) * P], ident[:, :])
                        tr.then_inc(xposed, 1)

        class Graph:

            def __init__(self, ctx, tag, dst, weighted, banks):
                self.dst, self.weighted, self.banks, self.tag, self.regs = dst, weighted, banks, tag, []
                self.hot_key = sb(ctx, "hot_key" + tag, [P, 2, KW, SUB], BF16)
                self.hot_src = sb(ctx, "hot_src" + tag, [P, 2, P, SUB], BF16)
                self.hot_w = sb(ctx, "hot_w" + tag, [P, 2, 3, P, SUB], BF16) if weighted else None
                self.rows, self.hot, self.cells, self.added = sems(
                    ctx, *(n + tag for n in ("hot_rows", "hot", "cells", "added")))

            def make(self, dve, q, p):
                after(dve, self.cells, q - 1)
                one_hot(dve, self.hot_src[:, p, :, :], srow[:, ds(q, 1), :], P).then_inc(self.rows, 1)
                hk = one_hot(dve, self.hot_key[:, p, :, :], key[:, ds(q, 1), :], KW)
                if self.weighted:
                    dve.wait_ge(self.rows, q + 1)
                    hk = weigh(dve, self.hot_w[:, p, :, :, :], self.hot_src[:, p, :, :], q)
                hk.then_inc(self.hot, 1)

            def bases(self, dve, q, n):
                regs = self.regs[0:n]
                dve.reg_load(regs, base_row[0:1, ds(q, n)])
                return [dve.snap(r, min_val=0, max_val=NP) for r in regs]

            def add(self, dve, q, p, base):
                dve.wait_ge(self.cells, q + 1)
                after(dve, self.added, q)
                window = self.dst[:, :, ds(base, W)]
                dve.tensor_tensor(window, window, self.banks[p][:, 0:KW].rearrange("p (b w) -> p b w", w=W),
                                  ALU.add).then_inc(self.added, 1)

            def sums(self, dve, q, n, last=False):
                if not self.regs:
                    self.regs.extend(dve.alloc_register(f"first_dst{i}{self.tag}") for i in range(LOADS))
                for i in range(n):
                    if not (last and i == n - 1):
                        self.make(dve, q + (i + 1), (i + 1) % 2)
                    if i % LOADS == 0:
                        base = self.bases(dve, q + i, min(LOADS, n - i))
                    self.add(dve, q + i, i % 2, base[i % LOADS])

            def products(self, pe, q, n):
                for i in range(n):
                    self.multiply(pe, q + i, i % 2)

            def multiply(self, pe, q, p):
                pe.wait_ge(self.hot, q + 1)
                after(pe, self.added, q - 1)
                mm = edge_product(pe, self.banks[p], self.hot_w[:, p, :, :, :] if self.weighted else
                                  self.hot_src[:, p, :, :].unsqueeze(1), self.hot_key[:, p, :, :])
                mm.then_inc(self.cells, 1)

        def general_passes(tag, dst, weighted):
            with ExitStack() as ctx:
                hot_key = sb(ctx, "ghot_key" + tag, [P, KW, SUB], BF16)
                hot_src = sb(ctx, "ghot_src" + tag, [P, P, SUB], BF16)
                hot_w = sb(ctx, "ghot_w" + tag, [P, 3, P, SUB], BF16) if weighted else None
                relp = sb(ctx, "relp" + tag, [Q, CE])
                keyp = sb(ctx, "keyp" + tag, [Q, CE])
                past = sb(ctx, "pastp" + tag, [Q, CE])
                keycol = sb(ctx, "keycol" + tag, [P, Q, SUB], BF16)
                firstp = sb(ctx, "firstp" + tag, [1, Q])
                basep = sb(ctx, "basep" + tag, [1, Q], I32)
                step, keys, keys_T, rows, hot, cells, added = sems(
                    ctx, *(n + tag for n in ("gstep", "gkeys", "gkeys_T", "grows", "ghot", "gcells", "gadded")))
                block = ctx.enter_context(nc.Block())
                SP_ = 7

                @block.vector
                def _(dve):
                    wide = dve.value_load(flag[0:1, 0:1], min_val=0, max_val=1)
                    with dve.If(wide > 0):
                        ch = Chain(dve, step)
                        ch.mark(dve.tensor_copy(relp[:, :], rel[:, :]))
                        ch.mark(dve.tensor_copy(firstp[:, :], first[:, :]))
                        with dve.Fori(0, PASSES - 1) as n:
                            ch.at(n * SP_ + 2)
                            ch.wait()
                            ch.mark(dve.tensor_scalar(relp[:, :], relp[:, :], float(W), None, ALU.subtract))
                            ch.mark(dve.tensor_scalar(firstp[:, :], firstp[:, :], float(W), float(NP), ALU.add, ALU.min))
                            ch.wait()
                            ch.mark(dve.tensor_copy(basep[:, :], firstp[:, :]))
                            ch.mark(dve.tensor_scalar(past[:, :], relp[:, :], float(W), FAR, ALU.is_ge, ALU.mult))
                            ch.mark(dve.tensor_tensor(keyp[:, :], sbw[:, :], relp[:, :], ALU.add))
                            ch.wait()
                            ch.mark(dve.tensor_tensor(keyp[:, :], keyp[:, :], past[:, :], ALU.add))
                            ch.wait()
                            ch.mark(dve.tensor_scalar(past[:, :], relp[:, :], 0.0, FAR, ALU.is_lt, ALU.mult))
                            ch.wait()
                            assert ch.n == SP_
                            dve.tensor_tensor(keyp[:, :], keyp[:, :], past[:, :], ALU.add).then_inc(keys, 1)
                            dve.wait_ge(keys_T, n + 1)
                            dve.tensor_copy(keycol[:, :, :],
                                            PS[1][:, 0:SUB * Q].rearrange("p (j q) -> p q j", j=SUB)).then_inc(keys, 1)
                            with dve.Fori(0, Q) as q:
                                dve.wait_ge(keys, 2 * n + 2)
                                one_hot(dve, hot_src[:, :, :], srow[:, ds(q, 1), :], P).then_inc(rows, 1)
                                h = one_hot(dve, hot_key[:, :, :], keycol[:, ds(q, 1), :], KW)
                                if weighted:
                                    dve.wait_ge(rows, n * Q + q + 1)
                                    h = weigh(dve, hot_w[:, :, :, :], hot_src[:, :, :], q)
                                h.then_inc(hot, 1)
                                base = dve.value_load(basep[0:1, ds(q, 1)], min_val=0, max_val=NP)
                                dve.wait_ge(cells, n * Q + q + 1)
                                window = dst[:, :, ds(base, W)]
                                dve.tensor_tensor(window, window, PS[0][:, 0:KW].rearrange("p (b w) -> p b w", w=W),
                                                  ALU.add).then_inc(added, 1)
                                dve.wait_ge(added, n * Q + q + 1)

                @block.tensor
                def _(pe):
                    wide = pe.value_load(flag[0:1, 0:1], min_val=0, max_val=1)
                    with pe.If(wide > 0):
                        with pe.Fori(0, PASSES - 1) as n:
                            pe.wait_ge(keys, 2 * n + 1)
                            for j in range(SUB):
                                tr = pe.transpose(PS[1][:, j * Q:(j + 1) * Q], keyp[:, j * P:(j + 1) * P], ident[0:Q, 0:Q])
                            tr.then_inc(keys_T, 1)
                            with pe.Fori(0, Q) as q:
                                pe.wait_ge(hot, n * Q + q + 1)
                                mm = edge_product(pe, PS[0], hot_w[:, :, :, :] if weighted else hot_src[:, :, :].unsqueeze(1),
                                                  hot_key[:, :, :])
                                mm.then_inc(cells, 1)

        with ExitStack() as g1:
            XT = sb(g1, "XT1", [P, KD, NP])
            HP = [sb(g1, f"HP{l}", [P, NT, D]) for l in range(2)]
            G = sb(g1, "G", [P, KD, NP])
            w_gate = [sb(g1, f"w_gate{l}", [P, KD, D]) for l in range(2)]
            w_gnn = [sb(g1, f"w_gnn{l}", [P, KD, D]) for l in range(2)]
            gnn_in = sems(g1, "gnn_w1_in", "gnn_w2_in")

            def self_loops(pool):
                pool.wait_ge(cleared, 1)
                for t in range(NT):
                    diag = C[:, t, t * P:(t + 1) * P]
                    pool.affine_select(out=diag, in_=diag, compare_op=ALU.not_equal, fill=1.0, base=0,
                                       pattern=[[-1, P]], channel_multiplier=1).then_inc(cleared, 1)

            def load_layer(sp, l):
                sp.dma_start(w_gate[l][:, :, :], a[f"gate_w{l + 1}"].rearrange("(k p) g -> p k g", p=P)).then_inc(gnn_in[l], 16)
                sp.dma_start(w_gnn[l][:, :, :], a[f"gnn_w{l + 1}"].rearrange("(k p) g -> p k g", p=P)).then_inc(gnn_in[l], 16)

            norm_phase("1", XT=XT, sync=lambda sp: [load_layer(sp, l) for l in range(2)], pool=self_loops)

            def gate_logits(pe, l, c, g, gate_mm, gated, between=lambda k: None):
                for k in range(KD):
                    between(k)
                    if k == 0:
                        after(pe, gated, KD * c + g - 1)
                    m = pe.matmul(PS[4 + g % 2][:, 0:CH], w_gate[l][:, k, g * P:(g + 1) * P], XT[:, k, ds(c * CH, CH)],
                                  start=(k == 0), stop=(k == KD - 1))
                m.then_inc(gate_mm, 1)

            def gate_out(act, l, c, g, gate_mm, gated):
                col = BIAS_COLS[("gnn_br1", "gnn_br2")[l]] + g
                act.wait_ge(gate_mm, KD * c + g + 1)
                act.activation(G[:, g, ds(c * CH, CH)], PS[4 + g % 2][:, 0:CH], ACT.Sigmoid,
                               bias=bcol[:, col:col + 1]).then_inc(gated, 1)

            def project(pe, l, c, j, lhs, proj_mm, proj_saved, between=lambda k: None):
                for k in range(KD):
                    between(k)
                    if k == 0:
                        after(pe, proj_saved, TPC * (c - 1) + j + 1 if isinstance(c, int) else TPC * c + (j + 1 - TPC))
                    m = pe.matmul(PS[6 + j][:, :], lhs(k), w_gnn[l][:, k, :], start=(k == 0), stop=(k == KD - 1))
                m.then_inc(proj_mm, 1)

            with ExitStack() as ctx:
                zeros = sb(ctx, "zeros", [P, D])
                tile_T = sb(ctx, "tile_T", [P, TPC, KD, P])
                zeroed, gate_mm, gated, tile_ready, proj_mm, proj_saved = sems(
                    ctx, "zeroed", "gate_mm1", "gated1", "tile_ready", "proj_mm1", "proj_saved1")
                graph = Graph(ctx, "_c", C, False, (PS[2], PS[3]))
                block = ctx.enter_context(nc.Block())
                ROUND = 12
                assert Q % ROUND == 0

                @block.sync
                def _(sp):
                    sp.wait_ge(zeroed, 1)
                    for b in range(2):
                        sp.dma_start(routed[b].rearrange("(t p) d -> p t d", p=P),
                                     zeros[:, :].unsqueeze(1).to_broadcast([P, ST, D])).then_inc(cleared_slots, 16)
                    sp.wait_ge(cleared_slots, 32)

                @block.gpsimd
                def _(pool):
                    pool.memset(zeros[:, :], 0.0).then_inc(zeroed, 1)

                @block.vector
                def _(dve):
                    graph.make(dve, 0, 0)
                    dve.wait_ge(cleared, NT + 1)
                    graph.sums(dve, 0, ROUND)
                    with dve.Fori(1, Q // ROUND - 1) as i:
                        graph.sums(dve, i * ROUND, ROUND)
                    graph.sums(dve, Q - ROUND, ROUND, last=True)

                @block.scalar
                def _(act):
                    def chunk(c):
                        for j in range(TPC):
                            after(act, proj_mm, TPC * (c - 1) + j + 1 if isinstance(c, int) else TPC * c + (j + 1 - TPC))
                            act.copy(tile_T[:, j, :, :], XT[:, :, ds(c * CH + j * P, P)]).then_inc(tile_ready, 1)
                        for g in range(KD):
                            gate_out(act, 0, c, g, gate_mm, gated)
                        for j in range(TPC):
                            act.wait_ge(proj_mm, TPC * c + j + 1)
                            act.copy(tile_of(HP[0], TPC * c + j), PS[6 + j][:, :]).then_inc(proj_saved, 1)
                    looped(act, NC, chunk)

                @block.tensor
                def _(pe):
                    pe.wait_ge(gnn_in[0], 32)
                    PER = 3 * KD + KD * TPC
                    assert PER * NC <= Q and PER % 2 == 0

                    def chunk(c):
                        def edges(i):
                            graph.multiply(pe, PER * c + i, i % 2)
                        for g in range(KD):
                            gate_logits(pe, 0, c, g, gate_mm, gated, lambda k: edges(3 * g + k) if k < 3 else None)
                        for j in range(TPC):
                            def before(k):
                                edges(3 * KD + KD * j + k)
                                if k == 0:
                                    pe.wait_ge(tile_ready, TPC * c + j + 1)
                            project(pe, 0, c, j, lambda k: tile_T[:, j, k, :], proj_mm, proj_saved, before)
                    looped(pe, NC, chunk)
                    graph.products(pe, PER * NC, Q - PER * NC)
            general_passes("_c", C, False)

            dis_all = sb(g1, "dis_all", [P, NP])
            dis_col = sb(g1, "dis_col", [P, NT])
            with ExitStack() as ctx:
                PE_CH = 2
                deg_row = sb(ctx, "deg_row", [1, PE_CH * CH])
                tile_sum = sb(ctx, "tile_sum", [P, NC - PE_CH, CH])
                diag = sb(ctx, "dis_diag", [P, 2, P])
                deg_mm, deg_saved, tile_sums, col_mm, root, dis_ready, diags, all_mm, all_saved, scaled, scaled_act = sems(
                    ctx, "deg_mm", "deg_saved", "tile_sums", "deg_col_mm", "deg_root", "dis_ready", "dis_diags",
                    "dis_all_mm", "dis_all_saved", "scaled", "scaled_act")
                block = ctx.enter_context(nc.Block())

                @block.vector
                def _(dve):
                    for i in range(NC - PE_CH):
                        c = PE_CH + i
                        dve.tensor_reduce(tile_sum[:, i, :], C[:, :, c * CH:(c + 1) * CH].rearrange("p s d -> p d s"),
                                          AX.X, ALU.add).then_inc(tile_sums, 1)
                    dve.wait_ge(root, 1)
                    dve.reciprocal(dis_col[:, :], dis_col[:, :]).then_inc(dis_ready, 1)
                    dve.wait_ge(dis_ready, 1)
                    for t in range(NT):
                        after(dve, all_mm, t - 1)
                        dve.tensor_scalar(diag[:, t % 2, :], ident[:, :], dis_col[:, t:t + 1], None, ALU.mult).then_inc(diags, 1)
                    for t in range(0, NT, 2):
                        dve.tensor_scalar(HP[0][:, t, :], HP[0][:, t, :], dis_col[:, t:t + 1], None, ALU.mult).then_inc(scaled, 1)

                @block.tensor
                def _(pe):
                    for c in range(PE_CH):
                        for s in range(NT):
                            m = pe.matmul(PS[c][0:1, 0:CH], ones[:, 0:1], C[:, s, c * CH:(c + 1) * CH], start=(s == 0), stop=(s == NT - 1))
                        m.then_inc(deg_mm, 1)
                    pe.wait_ge(tile_sums, NC - PE_CH)
                    pe.wait_ge(deg_saved, PE_CH)
                    for t in range(NT):
                        i = t * P - PE_CH * CH
                        if i < 0:
                            m = pe.matmul(PS[2][:, t:t + 1], deg_row[:, t * P:(t + 1) * P], ones[0:1, 0:1], start=True, stop=True)
                        else:
                            m = pe.matmul(PS[2][:, t:t + 1], tile_sum[:, i // CH, i % CH:i % CH + P], ones[:, 0:1], start=True, stop=True)
                    m.then_inc(col_mm, 1)
                    for t in range(NT):
                        pe.wait_ge(diags, t + 1)
                        pe.matmul(PS[3 + t // 4][:, (t % 4) * P:(t % 4 + 1) * P], ones[:, :], diag[:, t % 2, :],
                                  start=True, stop=True).then_inc(all_mm, 1)

                @block.scalar
                def _(act):
                    for c in range(PE_CH):
                        act.wait_ge(deg_mm, c + 1)
                        act.copy(deg_row[:, c * CH:(c + 1) * CH], PS[c][0:1, 0:CH]).then_inc(deg_saved, 1)
                    act.wait_ge(col_mm, 1)
                    act.activation(dis_col[:, :], PS[2][:, 0:NT], ACT.Sqrt).then_inc(root, 1)
                    act.wait_ge(dis_ready, 1)
                    for t in range(1, NT, 2):
                        act.activation(HP[0][:, t, :], HP[0][:, t, :], ACT.Copy, scale=dis_col[:, t:t + 1]).then_inc(scaled_act, 1)
                    for i in range(0, NT, 4):
                        n = min(4, NT - i)
                        act.wait_ge(all_mm, i + n)
                        act.copy(dis_all[:, i * P:(i + n) * P], PS[3 + i // 4][:, 0:n * P]).then_inc(all_saved, 1)

            with ExitStack() as ctx:
                Y = sb(ctx, "Y", [P, 2, CH])
                mix = sb(ctx, "mix", [P, 2, CH])
                H = sb(ctx, "H", [P, KD, CH])
                agg_mm, y_done, mixed, relu = zip(*[
                    sems(ctx, *(f"{n}{l}" for n in ("agg_mm", "y_done", "mix_step", "relu_done"))) for l in range(2)])
                gate_mm, gated, proj_mm, proj_saved, turn, turned, stats_done = sems(
                    ctx, "gate_mm2", "gated2", "proj_mm2", "proj_saved2", "h_turn", "h_turned", "stats_done")
                split, = sems(ctx, "weight_split")
                relu_h = sems(ctx, "relu_h0")[0], relu[1]
                block = ctx.enter_context(nc.Block())
                MIX = 3

                @block.tensor
                def _(pe):
                    def aggregate(l, c, f):
                        after(pe, y_done[l], KD * c + f - 1)
                        for s in range(NT):
                            m = pe.matmul(PS[f % 2][:, 0:CH], HP[l][:, s, f * P:(f + 1) * P], C[:, s, ds(c * CH, CH)],
                                          start=(s == 0), stop=(s == NT - 1))
                        m.then_inc(agg_mm[l], 1)

                    def project_next(c):
                        pe.wait_ge(relu[0], KD * c + KD)
                        pe.wait_ge(relu_h[0], KD * c + KD)
                        for j in range(TPC):
                            project(pe, 1, c, j, lambda k: H[:, k, j * P:(j + 1) * P], proj_mm, proj_saved)

                    def gates_next(c):
                        for g in range(KD):
                            gate_logits(pe, 1, c, g, gate_mm, gated)

                    def turn_back(c):
                        pe.wait_ge(relu[1], KD * c + KD)
                        for j in range(TPC):
                            after(pe, turned, TPC * (c - 1) + j + 1 if isinstance(c, int) else TPC * c + (j + 1 - TPC))
                            for f in range(KD):
                                m = pe.transpose(PS[6 + j][:, f * P:(f + 1) * P], H[:, f, j * P:(j + 1) * P], ident[:, :])
                            m.then_inc(turn, 1)

                    def chunk(l, c, before):
                        aggregate(l, c, 0)
                        if l == 0:
                            project_next(before)
                        else:
                            turn_back(before)
                        for f in range(1, KD):
                            aggregate(l, c, f)
                        if l == 0:
                            gates_next(before)

                    pe.wait_ge(gnn_in[1], 32)
                    for l in range(2):
                        for f in range(KD):
                            aggregate(l, 0, f)
                        chunk(l, 1, 0)
                        with pe.Fori(2, NC) as c:
                            chunk(l, c, c - 1)
                        if l == 0:
                            project_next(NC - 1)
                            gates_next(NC - 1)
                            pe.wait_ge(proj_saved, NT)
                        else:
                            turn_back(NC - 1)

                @block.vector
                def _(dve):
                    def mix_out(l, c, f):
                        ch = Chain(dve, mixed[l])
                        ch.at(MIX * KD * c + MIX * f)
                        col = BIAS_COLS[("gnn_b1", "gnn_b2")[l]] + f
                        h, y, m = XT[:, f, ds(c * CH, CH)], Y[:, f % 2, :], mix[:, f % 2, :]
                        dve.wait_ge(agg_mm[l], KD * c + f + 1)
                        dve.tensor_tensor(y, PS[f % 2][:, 0:CH], dis_all[:, ds(c * CH, CH)], ALU.mult).then_inc(y_done[l], 1)
                        dve.wait_ge(y_done[l], KD * c + f + 1)
                        after(dve, relu[l], KD * c + f - 1)
                        ch.mark(dve.scalar_tensor_tensor(out=m, in0=y, scalar=bcol[:, col:col + 1], in1=h,
                                                         op0=ALU.add, op1=ALU.subtract))
                        ch.wait()
                        if l == 1:
                            dve.wait_ge(gated, KD * c + f + 1)
                        ch.mark(dve.tensor_tensor(m, m, G[:, f, ds(c * CH, CH)], ALU.mult))
                        ch.wait()
                        ch.mark(dve.tensor_tensor(m, m, h, ALU.add))

                    def back(c):
                        for j in range(TPC):
                            dve.wait_ge(turn, TPC * c + j + 1)
                            x_t = tile_of(X, TPC * c + j)
                            dve.tensor_tensor(x_t, x_t, PS[6 + j][:, :], ALU.add).then_inc(turned, 1)
                        for j in range(TPC):
                            dve.wait_ge(turned, TPC * c + j + 1)
                            dve.bn_stats(stats[:, ds(TPC * c + j, 1), :].rearrange("p a s -> p (a s)"),
                                         tile_of(X, TPC * c + j)).then_inc(stats_done, 1)

                    for m in range(3):
                        dve.tensor_copy(part[:, :, m, :], wexp[:, :, :]).then_inc(split, 1)
                        if m < 2:
                            dve.wait_ge(split, 2 * m + 1)
                            dve.tensor_tensor(wexp[:, :, :], wexp[:, :, :], part[:, :, m, :], ALU.subtract).then_inc(split, 1)
                            dve.wait_ge(split, 2 * m + 2)

                    for l in range(2):
                        for f in range(KD):
                            mix_out(l, 0, f)

                        def chunk(c, before):
                            mix_out(l, c, 0)
                            if l == 1:
                                back(before)
                            for f in range(1, KD):
                                mix_out(l, c, f)
                        chunk(1, 0)
                        with dve.Fori(2, NC) as c:
                            chunk(c, c - 1)
                    back(NC - 1)

                @block.scalar
                def _(act):
                    def relu_out(l, c, f):
                        act.wait_ge(mixed[l], MIX * KD * c + MIX * f + MIX)
                        after(act, (proj_mm, turn)[l], TPC * c)
                        act.activation(H[:, f, :], mix[:, f % 2, :], ACT.Relu).then_inc(relu_h[l], 1)
                        if l == 0:
                            act.activation(XT[:, f, ds(c * CH, CH)], mix[:, f % 2, :], ACT.Relu).then_inc(relu[0], 1)

                    def save_projected(c):
                        for j in range(TPC):
                            t = TPC * c + j
                            act.wait_ge(proj_mm, TPC * c + j + 1)
                            act.activation(tile_of(HP[1], t), PS[6 + j][:, :], ACT.Copy, scale=dis_col[:, ds(t, 1)]).then_inc(proj_saved, 1)

                    def gates(c):
                        for g in range(KD):
                            gate_out(act, 1, c, g, gate_mm, gated)

                    for f in range(KD):
                        relu_out(0, 0, f)

                    def chunk(c, before):
                        relu_out(0, c, 0)
                        save_projected(before)
                        for f in range(1, KD):
                            relu_out(0, c, f)
                        gates(before)
                    chunk(1, 0)
                    with act.Fori(2, NC) as c:
                        chunk(c, c - 1)
                    save_projected(NC - 1)
                    gates(NC - 1)
                    for f in range(KD):
                        relu_out(1, 0, f)
                    with act.Fori(1, NC) as c:
                        for f in range(KD):
                            relu_out(1, c, f)
        nc.gpsimd.sem_clear(range(first_reused, relu_h[0].num + 1))
        nc.all_engine_barrier()
        scope1.close()

        A = sb(top, "A", [P, NT, CW])
        slot = sb(top, "slot", [P, 2 * NT], I32)
        gate = sb(top, "gate", [P, 2 * NT])
        gated_hot = sb(top, "gated_hot", [32, NP])
        bias2 = sb(top, "bias2", [2 * NE + 1, D])
        bias2_in, = sems(top, "bias2_in")
        with ExitStack() as g2:
            FIRST_Q, SHARED_Q, TILE_Q = 2 * NC, 4, 2
            assert SHARED_Q == 2 * 2
            _left = Q - FIRST_Q - SHARED_Q * (NC - 1) - 2 * TILE_Q * (ST - 2)
            assert _left >= 0 and _left % 2 == 0
            BANK_Q = 16, _left - 16
            q_bank = [FIRST_Q + SHARED_Q * (NC - 1)]
            q_bank.append(q_bank[0] + BANK_Q[0] + TILE_Q * (ST - 2))
            graph = Graph(g2, "_a", A, True, (PS[0], PS[1]))
            a_cleared, = sems(g2, "a_cleared")
            tile_expert = sb(g2, "tile_expert", [1, 2 * ST], I32)
            passed = sb(g2, "passed", [1, NE], I32)
            W1 = [sb(g2, "W1_0", [P, NE * KD * FF]), None]
            w1_in, w2_in, w2_again, scattered = sems(g2, "expert_w1_in", "expert_w2_in", "expert_w2_again", "scattered")

            def load_w1(sp, b):
                tag = ("sp", "fq")[b]
                for e in range(NE):
                    sp.dma_start(W1[b][:, e * KD * FF:(e + 1) * KD * FF].rearrange("p (k f) -> p k f", k=KD),
                                 a[f"W1_{tag}"][e].rearrange("(k p) f -> p k f", p=P)).then_inc(w1_in, 16)

            def load_w2(sp, b, W2, free=None):
                tag = ("sp", "fq")[b]
                for e in range(NE):
                    if b == 1:
                        free(e)
                    sp.dma_start(W2[:, e * 2 * D:(e + 1) * 2 * D].rearrange("p (f d) -> p f d", f=2),
                                 a[f"W2_{tag}"][e].rearrange("(f p) d -> p f d", p=P)).then_inc((w2_in, w2_again)[b], 16)

            with ExitStack() as ctx2:
                XT = sb(ctx2, "XT2", [P, KD, NP])
                Xn = sb(ctx2, "Xn2", [P, NT, D])

                ws1 = sb(ctx2, "ws1", [P, KD, FF])
                ws2 = sb(ctx2, "ws2", [P, 2, D])
                wr = sb(ctx2, "wr", [P, KD, 2 * NE])
                br = sb(ctx2, "br", [2 * NE, 1])
                sw_in, = sems(ctx2, "shared_w_in")

                def early(sp):
                    sp.dma_start(wr[:, :, :], a["router_w"].rearrange("(k p) e -> p k e", p=P)).then_inc(sw_in, 16)
                    sp.dma_start(br[:, :], a["router_b"]).then_inc(sw_in, 16)
                    sp.dma_start(ws1[:, :, :], a["ws1"].rearrange("(k p) f -> p k f", p=P)).then_inc(sw_in, 16)
                    sp.dma_start(ws2[:, :, :], a["ws2"].rearrange("(f p) d -> p f d", p=P)).then_inc(sw_in, 16)
                    sp.dma_start(bias2[:, :], a["b2_all"]).then_inc(bias2_in, 16)
                    load_w1(sp, 0)
                norm_phase("2", Xn=Xn, XT=XT, sync=early, have_stats=True,
                           pool=lambda pool: pool.memset(A[:, :, :], 0.0).then_inc(a_cleared, 1))

                LT = sb(ctx2, "LT", [2 * NE, NP])
                HS = sb(ctx2, "HS", [P, 2, CH])
                L = sb(ctx2, "L", [P, 2 * NT, NE])
                ex = sb(ctx2, "ex", [P, 2 * NT, NE])
                hotx = sb(ctx2, "hotx", [P, 2 * NT, NE])
                col = sb(ctx2, "col", [P, 4, 2 * NT])
                rev = sb(ctx2, "rev", [P, NE])
                real = sb(ctx2, "real", [P, 1])
                tri = sb(ctx2, "tri", [P, P])
                run = sb(ctx2, "run", [P, NT + 1, 2 * NE])
                thresholds = sb(ctx2, "thresholds", [P, NT])
                tiles_gt = sb(ctx2, "tiles_gt", [P, 2 * NE, NT])
                tiles = sb(ctx2, "tiles", [P, 2, NE])
                start = sb(ctx2, "start", [P, 2, NE + 1])
                start_row = sb(ctx2, "start_row", [P, 2 * NE])
                slotf = sb(ctx2, "slotf", [P, 2 * NT])
                tile_no = sb(ctx2, "tile_no", [1, ST])
                past = sb(ctx2, "pastt", [1, ST, NE])
                chosen = sb(ctx2, "chosen", [1, 2, ST])
                (rmm, routed_T, rT, lt, step, expd, hot_ready, prefix, slots_ready, ghot_T, ghot, s1, hs, s2, xadd,
                 rconst, tri1) = sems(
                    ctx2, "router_mm", "logits_T", "logits_turned", "logits", "route_step", "route_exp",
                    "hot_ready", "prefix_mm", "slots_ready", "gated_hot_T", "gated_hot_saved", "shared1_mm", "shared_h",
                    "shared2_mm", "shared_added", "route_consts", "tri_ones")
                block = ctx2.enter_context(nc.Block())

                @block.gpsimd
                def _(pool):
                    pool.memset(tri[:, :], 1.0).then_inc(tri1, 1)
                    pool.iota(rev[:, :], pattern=[[-1, NE]], base=NE, channel_multiplier=0,
                              allow_small_or_imprecise_dtypes=True).then_inc(rconst, 1)
                    pool.memset(real[:, :], 1.0).then_inc(tri1, 1)
                    pool.iota(thresholds[:, :], pattern=[[P, NT]], base=0, channel_multiplier=0,
                              allow_small_or_imprecise_dtypes=True).then_inc(rconst, 1)
                    pool.iota(tile_no[:, :], pattern=[[1, ST]], base=0, channel_multiplier=0,
                              allow_small_or_imprecise_dtypes=True).then_inc(rconst, 1)
                    pool.memset(gated_hot[:, :], 1.0).then_inc(rconst, 1)
                    pool.memset(run[:, 0, :], 0.0).then_inc(rconst, 1)
                    pool.memset(start[:, :, :], 0.0).then_inc(rconst, 1)
                    pool.wait_ge(tri1, 2)
                    pool.affine_select(out=tri[:, :], in_=tri[:, :], compare_op=ALU.is_ge, fill=0.0, base=-1,
                                       pattern=[[1, P]], channel_multiplier=-1).then_inc(rconst, 1)
                    pool.affine_select(out=real[:, :], in_=real[:, :], compare_op=ALU.is_ge, fill=0.0, base=LAST - 1,
                                       pattern=[[0, 1]], channel_multiplier=-1).then_inc(rconst, 1)
                    pool.wait_ge(slots_ready, 1)
                    pool.wait_ge(cleared_slots, 32)
                    for t in range(NT):
                        n = P if t < NT - 1 else LAST
                        for b in range(2):
                            pool.indirect_dma_start(
                                routed[b], bass.IndirectOffsetOnAxis(ap=slot[0:n, 2 * t + b:2 * t + b + 1], axis=0),
                                Xn[0:n, t, :], None).then_inc(scattered, 16)
                    pool.wait_ge(scattered, 2 * NT * 16)

                @block.tensor
                def _(pe):
                    pe.wait_ge(sw_in, 64)

                    def router(c):
                        after(pe, lt, c)
                        for k in range(KD):
                            if k % 2 == 0:
                                graph.multiply(pe, 2 * c + k // 2, k // 2)
                            m = pe.matmul(PS[6][0:2 * NE, 0:CH], wr[:, k, :], XT[:, k, ds(c * CH, CH)],
                                          start=(k == 0), stop=(k == KD - 1))
                        m.then_inc(rmm, 1)
                    looped(pe, NC, router)
                    pe.wait_ge(lt, NC)
                    for t in range(NT):
                        m = pe.transpose(PS[7][:, 2 * NE * t:2 * NE * (t + 1)], LT[:, t * P:(t + 1) * P], ident[0:2 * NE, 0:2 * NE])
                    m.then_inc(rT, 1)

                    def shared(c, edges=None):
                        after(pe, hs, 2 * c)
                        for f in range(2):
                            for k in range(KD):
                                if edges is not None and k % 2 == 0:
                                    graph.multiply(pe, edges + 2 * f + k // 2, k // 2)
                                m = pe.matmul(PS[2 + f][:, 0:CH], ws1[:, k, f * P:(f + 1) * P], XT[:, k, ds(c * CH, CH)],
                                              start=(k == 0), stop=(k == KD - 1))
                            m.then_inc(s1, 1)
                        pe.wait_ge(hs, 2 * c + 2)
                        for j in range(TPC):
                            after(pe, xadd, TPC * (c - 1) + j + 1 if isinstance(c, int) else TPC * c + (j + 1 - TPC))
                            for f in range(2):
                                m = pe.matmul(PS[4 + j][:, :], HS[:, f, j * P:(j + 1) * P], ws2[:, f, :],
                                              start=(f == 0), stop=(f == 1))
                            m.then_inc(s2, 1)
                    shared(0)
                    pe.wait_ge(hot_ready, 1)
                    flat = hotx[:, :, :].rearrange("p t e -> p (t e)")
                    pe.matmul(PS[6][:, 0:2 * NT * NE], tri[:, :], flat, start=True, stop=True).then_inc(prefix, 1)
                    pe.matmul(PS[7][:, 0:2 * NT * NE], ones[:, :], flat, start=True, stop=True).then_inc(prefix, 1)
                    with pe.Fori(1, NC) as c:
                        edges = SHARED_Q * c + (FIRST_Q - SHARED_Q)
                        shared(c, edges)
                    pe.wait_ge(ghot_T, 1)
                    pe.wait_ge(graph.added, q_bank[0])
                    for t in range(NT):
                        bank = t // 4
                        m = pe.transpose(PS[(0, 1, 6)[bank]][0:2 * NE, (t % 4) * P:(t % 4 + 1) * P],
                                         ex[:, 2 * t:2 * t + 2, :].rearrange("p t e -> p (t e)"), ident[:, :])
                    m.then_inc(routed_T, 1)

                @block.scalar
                def _(act):
                    def logits(c):
                        act.wait_ge(rmm, c + 1)
                        act.activation(LT[:, ds(c * CH, CH)], PS[6][0:2 * NE, 0:CH], ACT.Identity, bias=br[:, 0:1]).then_inc(lt, 1)
                    looped(act, NC, logits)

                    def shared(c):
                        for f in range(2):
                            act.wait_ge(s1, 2 * c + f + 1)
                            after(act, s2, TPC * c)
                            act.activation(HS[:, f, :], PS[2 + f][:, 0:CH], ACT.Gelu,
                                           bias=bcol[:, BIAS_COLS["bs1"] + f:BIAS_COLS["bs1"] + f + 1]).then_inc(hs, 1)
                    act.wait_ge(expd, 1)
                    act.activation(ex[:, :, :], L[:, :, :], ACT.Exp).then_inc(expd, 1)
                    looped(act, NC, shared)
                    act.wait_ge(routed_T, 1)
                    for i, bank in enumerate((0, 1, 6)):
                        w = min(4, NT - 4 * i) * P
                        act.copy(gated_hot[0:2 * NE, 4 * i * P:4 * i * P + w], PS[bank][0:2 * NE, 0:w]).then_inc(ghot, 1)

                @block.vector
                def _(dve):
                    ch = Chain(dve, step)
                    tt, tsc = dve.tensor_tensor, dve.tensor_scalar

                    def over(c2):
                        return c2.unsqueeze(2).to_broadcast([P, 2 * NT, NE])
                    graph.make(dve, 0, 0)
                    dve.wait_ge(a_cleared, 1)
                    graph.sums(dve, 0, 2)
                    with dve.Fori(1, NC) as c:
                        graph.sums(dve, 2 * c, 2)
                    dve.wait_ge(rT, 1)
                    dve.wait_ge(rconst, 8)
                    ch.mark(dve.tensor_copy(L[:, :, :], PS[7][:, 0:2 * NT * NE].rearrange("p (t e) -> p t e", e=NE)))
                    ch.wait()
                    ch.mark(dve.tensor_reduce(col[:, 0, :], L[:, :, :], AX.X, ALU.max))
                    ch.wait()
                    tt(L[:, :, :], L[:, :, :], over(col[:, 0, :]), ALU.subtract).then_inc(expd, 1)
                    dve.wait_ge(expd, 2)
                    ch.mark(dve.tensor_reduce(col[:, 1, :], ex[:, :, :], AX.X, ALU.add))
                    ch.mark(dve.tensor_reduce(col[:, 2, :], ex[:, :, :], AX.X, ALU.max))
                    ch.wait()
                    ch.mark(dve.reciprocal(gate[:, :], col[:, 1, :]))
                    ch.mark(tt(L[:, :, :], ex[:, :, :], over(col[:, 2, :]), ALU.is_equal))
                    ch.wait()
                    ch.mark(tt(gate[:, :], gate[:, :], col[:, 2, :], ALU.mult))
                    ch.mark(tt(L[:, :, :], L[:, :, :], rev[:, :].unsqueeze(1).to_broadcast([P, 2 * NT, NE]), ALU.mult))
                    ch.wait()
                    ch.mark(dve.tensor_reduce(col[:, 3, :], L[:, :, :], AX.X, ALU.max))
                    ch.wait()
                    ch.mark(tt(hotx[:, :, :], L[:, :, :], over(col[:, 3, :]), ALU.is_equal))
                    ch.wait()
                    tsc(hotx[:, 2 * NT - 2:2 * NT, :], hotx[:, 2 * NT - 2:2 * NT, :], real[:, 0:1], None, ALU.mult).then_inc(hot_ready, 1)
                    dve.wait_ge(hot_ready, 1)
                    tt(ex[:, :, :], hotx[:, :, :], over(gate[:, :]), ALU.mult).then_inc(ghot_T, 1)
                    dve.wait_ge(prefix, 2)
                    for t in range(NT):
                        ch.mark(tt(run[:, t + 1, :], run[:, t, :], PS[7][:, 2 * NE * t:2 * NE * (t + 1)], ALU.add))
                        ch.wait()
                    ch.mark(tt(tiles_gt[:, :, :], run[:, NT, :].unsqueeze(2).to_broadcast([P, 2 * NE, NT]),
                               thresholds[:, :].unsqueeze(1).to_broadcast([P, 2 * NE, NT]), ALU.is_gt))
                    ch.wait()
                    ch.mark(dve.tensor_reduce(tiles[:, :, :].rearrange("p b e -> p (b e)"), tiles_gt[:, :, :], AX.X, ALU.add))
                    for e in range(NE):
                        ch.wait()
                        ch.mark(tt(start[:, :, e + 1], start[:, :, e], tiles[:, :, e], ALU.add))
                    ch.wait()
                    ch.mark(tsc(start_row[:, :].rearrange("p (b e) -> p b e", b=2), start[:, :, 0:NE], float(P), None, ALU.mult))
                    Lv = L[:, :, :].rearrange("p (t b) e -> p t (b e)", b=2)
                    ch.mark(tt(Lv, PS[6][:, 0:2 * NT * NE].rearrange("p (t e) -> p t e", t=NT), run[:, 0:NT, :], ALU.add))
                    ch.wait()
                    ch.mark(tt(Lv, Lv, start_row[:, :].unsqueeze(1).to_broadcast([P, NT, 2 * NE]), ALU.add))
                    ch.wait()
                    ch.mark(tt(L[:, :, :], L[:, :, :], hotx[:, :, :], ALU.mult))
                    ch.wait()
                    ch.mark(dve.tensor_reduce(slotf[:, :], L[:, :, :], AX.X, ALU.add))
                    ch.wait()
                    dve.tensor_copy(slot[:, :], slotf[:, :]).then_inc(slots_ready, 1)
                    for b in range(2):
                        ch.mark(tt(past[:, :, :], tile_no[:, :].unsqueeze(2).to_broadcast([1, ST, NE]),
                                   start[0:1, b, 1:NE + 1].unsqueeze(1).to_broadcast([1, ST, NE]), ALU.is_ge))
                        ch.wait()
                        ch.mark(dve.tensor_reduce(chosen[:, b, :], past[:, :, :], AX.X, ALU.add))
                        ch.wait()
                    ch.mark(tsc(passed[:, :], start[0:1, 0, 1:NE + 1], 1.0, float(ST), ALU.add, ALU.min))
                    ch.mark(tsc(tile_expert[:, :], chosen[:, :, :].rearrange("p b t -> p (b t)"), float(NE - 1), None, ALU.min))
                    ch.wait()

                    def shared(c):
                        for j in range(TPC):
                            dve.wait_ge(s2, TPC * c + j + 1)
                            x_t = tile_of(X, TPC * c + j)
                            tt(x_t, x_t, PS[4 + j][:, :], ALU.add).then_inc(xadd, 1)
                    shared(0)
                    with dve.Fori(1, NC) as c:
                        graph.sums(dve, SHARED_Q * c + (FIRST_Q - SHARED_Q), SHARED_Q)
                        shared(c)

            with ExitStack() as ctx2:
                W1[1] = sb(ctx2, "W1_1", [P, NE * KD * FF])
                W2 = sb(ctx2, "W2", [P, NE * 2 * D])
                idle_e = sb(ctx2, "idle_e", [1, NE])
                graph.banks = PS[4], PS[5]
                xg = sb(ctx2, "xg", [P, D])
                xgT = sb(ctx2, "xgT", [P, KD, P])
                b1 = sb(ctx2, "b1", [P, NE * FF])
                h = sb(ctx2, "h", [P, FF])
                hT = sb(ctx2, "hT", [P, 2, P])
                yo = sb(ctx2, "yo", [P, D])
                per = [sems(ctx2, *(f"{n}{b}" for n in ("xg_in", "xg_T", "xgT_saved", "up_mm", "h_sum", "h_gelu",
                                                        "h_T", "hT_saved", "down_mm", "y_saved", "y_out"))) for b in range(2)]
                b1_in, b1_again = sems(ctx2, "b1_in", "b1_again")
                block = ctx2.enter_context(nc.Block())

                def load_b1(sp):
                    sp.dma_start(b1[:, :], a["b1_sp"].rearrange("e f -> (e f)").unsqueeze(0).to_broadcast(
                        [P, NE * FF])).then_inc(b1_in, 16)

                @block.gpsimd
                def _(pool):
                    def free(e):
                        if e < NE - 1:
                            pool.wait_ge(per[0][8], pool.value_load(passed[0:1, e:e + 1], min_val=1, max_val=ST))
                            pool.tensor_tensor(idle_e[:, e:e + 1], eps[0:1, :], eps[0:1, :], ALU.add)
                        else:
                            pool.wait_ge(per[0][8], ST)
                        pool.dma_start(b1[:, e * FF:(e + 1) * FF],
                                       a["b1_fq"][e:e + 1, :].to_broadcast([P, FF])).then_inc(b1_again, 16)
                    load_w2(pool, 1, W2, free)

                @block.sync
                def _(sp):
                    for b in range(2):
                        xg_in, xg_T, xgT_saved, up_mm, h_sum, h_gelu, h_T, hT_saved, down_mm, y_saved, y_out = per[b]

                        def load_x(j):
                            after(sp, xg_T, j)
                            sp.dma_start(xg[:, :], routed[b][ds(j * P, P), :]).then_inc(xg_in, 16)

                        def store(j):
                            sp.wait_ge(y_saved, j + 1)
                            sp.dma_start(expert_out[b][ds(j * P, P), :], yo[:, :]).then_inc(y_out, 16)

                        if b == 1:
                            sp.wait_ge(per[0][1], ST)
                        load_x(0)
                        if b == 0:
                            load_b1(sp)
                            load_w2(sp, 0, W2)
                        for j in range(1, 3):
                            load_x(j)
                        if b == 0:
                            with sp.Fori(3, 3 + NE) as j:
                                load_x(j)
                                sp.dma_start(W1[1][:, ds(j * (KD * FF) - 3 * KD * FF, KD * FF)].rearrange("p (k f) -> p k f", k=KD),
                                             a["W1_fq"][ds(j - 3, 1)].rearrange("a (k p) f -> p (a k) f", p=P)).then_inc(w1_in, 16)
                                store(j - 3)
                        with sp.Fori(3 + NE if b == 0 else 3, ST) as j:
                            load_x(j)
                            store(j - 3)
                        for j in range(ST - 3, ST):
                            store(j)
                        sp.wait_ge(y_out, 16 * ST)

                @block.tensor
                def _(pe):
                    for b in range(2):
                        xg_in, xg_T, xgT_saved, up_mm, h_sum, h_gelu, h_T, hT_saved, down_mm, y_saved, y_out = per[b]

                        def turn_x(j):
                            pe.wait_ge(xg_in, 16 * (j + 1))
                            after(pe, xgT_saved, j)
                            for k in range(KD):
                                m = pe.transpose(PS[1][:, k * P:(k + 1) * P], xg[:, k * P:(k + 1) * P], ident[:, :])
                            m.then_inc(xg_T, 1)

                        def up(j):
                            e = pe.value_load(tile_expert[0:1, ds(b * ST + j, 1)], min_val=0, max_val=NE - 1)
                            pe.wait_ge(xgT_saved, j + 1)
                            after(pe, h_sum, j)
                            for k in range(KD):
                                m = pe.matmul(PS[0][:, 0:FF], xgT[:, k, :], W1[b][:, ds(e * (KD * FF) + k * FF, FF)],
                                              start=(k == 0), stop=(k == KD - 1))
                            m.then_inc(up_mm, 1)

                        def turn_h(j):
                            pe.wait_ge(h_gelu, j + 1)
                            after(pe, hT_saved, j)
                            for f in range(2):
                                m = pe.transpose(PS[3][:, f * P:(f + 1) * P], h[:, f * P:(f + 1) * P], ident[:, :])
                            m.then_inc(h_T, 1)

                        def down(j):
                            e = pe.value_load(tile_expert[0:1, ds(b * ST + j, 1)], min_val=0, max_val=NE - 1)
                            pe.wait_ge(hT_saved, j + 1)
                            after(pe, y_saved, j)
                            for f in range(2):
                                m = pe.matmul(PS[2][:, :], hT[:, f, :], W2[:, ds(e * (2 * D) + f * D, D)],
                                              start=(f == 0), stop=(f == 1))
                            m.then_inc(down_mm, 1)

                        graph.products(pe, q_bank[b], BANK_Q[b])
                        qt = q_bank[b] + BANK_Q[b] - TILE_Q
                        pe.wait_ge(w1_in, 16 * NE * (b + 1))
                        if b == 1:
                            pe.wait_ge(per[0][9], ST)
                            pe.wait_ge(per[0][7], ST)
                        turn_x(0)
                        up(0)
                        turn_x(1)
                        turn_h(0)
                        pe.wait_ge((w2_in, w2_again)[b], 16 * NE)
                        with pe.Fori(1, ST - 1) as j:
                            up(j)
                            turn_x(j + 1)
                            graph.multiply(pe, TILE_Q * j + qt, 0)
                            down(j - 1)
                            turn_h(j)
                            graph.multiply(pe, TILE_Q * j + (qt + 1), 1)
                        up(ST - 1)
                        down(ST - 2)
                        turn_h(ST - 1)
                        down(ST - 1)

                @block.vector
                def _(dve):
                    for b in range(2):
                        xg_in, xg_T, xgT_saved, up_mm, h_sum, h_gelu, h_T, hT_saved, down_mm, y_saved, y_out = per[b]

                        def bias(j):
                            e = dve.value_load(tile_expert[0:1, ds(b * ST + j, 1)], min_val=0, max_val=NE - 1)
                            dve.wait_ge(up_mm, j + 1)
                            after(dve, h_T, j)
                            if b == 1 and isinstance(j, int) and j == 0:
                                dve.wait_ge(per[0][6], ST)
                            dve.tensor_tensor(h[:, :], PS[0][:, 0:FF], b1[:, ds(e * FF, FF)], ALU.add).then_inc(h_sum, 1)
                        graph.sums(dve, q_bank[b], BANK_Q[b])
                        qt = q_bank[b] + BANK_Q[b] - TILE_Q
                        dve.wait_ge(*((b1_in, 16) if b == 0 else (b1_again, 16 * NE)))
                        bias(0)
                        with dve.Fori(1, ST - 2) as j:
                            bias(j)
                            graph.sums(dve, TILE_Q * j + qt, TILE_Q)
                        bias(ST - 2)
                        graph.sums(dve, TILE_Q * (ST - 2) + qt, TILE_Q, last=b == 1)
                        bias(ST - 1)

                @block.scalar
                def _(act):
                    for b in range(2):
                        xg_in, xg_T, xgT_saved, up_mm, h_sum, h_gelu, h_T, hT_saved, down_mm, y_saved, y_out = per[b]

                        def save_x(j):
                            act.wait_ge(xg_T, j + 1)
                            after(act, up_mm, j)
                            act.copy(xgT[:, :, :].rearrange("p k n -> p (k n)"), PS[1][:, :]).then_inc(xgT_saved, 1)

                        def gelu(j):
                            act.wait_ge(h_sum, j + 1)
                            act.activation(h[:, :], h[:, :], ACT.Gelu).then_inc(h_gelu, 1)

                        def save_h(j):
                            act.wait_ge(h_T, j + 1)
                            after(act, down_mm, j)
                            act.copy(hT[:, :, :].rearrange("p f n -> p (f n)"), PS[3][:, 0:FF]).then_inc(hT_saved, 1)

                        def save_y(j):
                            act.wait_ge(down_mm, j + 1)
                            after(act, y_out, 16 * j)
                            act.copy(yo[:, :], PS[2][:, :]).then_inc(y_saved, 1)
                        save_x(0)
                        save_x(1)
                        gelu(0)
                        save_h(0)
                        if b == 1:
                            act.wait_ge(per[0][10], 16 * ST)
                        with act.Fori(1, ST - 1) as j:
                            gelu(j)
                            save_x(j + 1)
                            save_y(j - 1)
                            save_h(j)
                        gelu(ST - 1)
                        save_y(ST - 2)
                        save_h(ST - 1)
                        save_y(ST - 1)


        with ExitStack() as g3:
            AT = sb(g3, "AT", [P, NT, NP])
            M = [sb(g3, f"M{i}", [P, NT, P]) for i in range(2)]
            valid = sb(g3, "valid", [P, NT])
            inv = sb(g3, "inv", [P, NT])
            inv_all = sb(g3, "inv_all", [P, NP])
            wm = sb(g3, "wm", [P, KD, FF])
            w1 = sb(g3, "l1_w1", [P, KD, P])
            w2 = sb(g3, "l1_w2", [P, D])
            rows3 = sb(g3, "rows3", [P, NROW])
            w3_in, = sems(g3, "block3_w_in")

            def bias_row(name):
                at, n = BIAS_ROWS[name]
                return rows3[:, at:at + n]

            general_passes("_a", A, True)
            with ExitStack() as ctx:
                RING = 4
                back = sb(ctx, "back", [P, RING, 2, D])
                total = sb(ctx, "total", [P, NT])
                diag = sb(ctx, "diag", [P, 2, P])
                unused = sb(ctx, "unused", [P, NP])
                staged = sb(ctx, "staged3", [P, 2, D])
                turned_x = sb(ctx, "turned_x", [P, 2, KD, P])
                MT = sb(ctx, "MT", [P, 2, 2, P])
                got = sems(ctx, *(f"got{t}" for t in range(NT)))
                (bias_mm, step, sums, turned, saved, act_saved, inv_step, valid_done, diags, rows_mm, rows_saved) = sems(
                    ctx, "bias_mm", "combine_step", "row_sums", "a_turned", "at_saved", "at_saved_act", "inv_step",
                    "valid_done", "diags", "inv_rows_mm", "inv_rows_saved")
                aggr, root, rstd_done, normed, x_turned, x_saved, mt_mm, mt_saved, m_mm, m_saved = sems(
                    ctx, "aggr3", "root_x3", "rstd3", "normed3", "x_turned", "x_saved", "mt_mm", "mt_saved", "m_mm", "m_saved")
                block = ctx.enter_context(nc.Block())
                TS = 4
                BIAS_PS, X_PS, MT_PS, M_PS, INV_PS = PS[3], PS[4], PS[5], PS[6], (PS[0], PS[1], PS[2])

                def rows(t):
                    return P if t < NT - 1 else LAST

                @block.sync
                def _(sp):
                    sp.dma_start(wm[:, :, :], a["wm"].rearrange("(k p) f -> p k f", p=P)).then_inc(w3_in, 16)
                    sp.dma_start(w1[:, :, :], a["l1_w1"].rearrange("(k p) f -> p k f", p=P)).then_inc(w3_in, 16)
                    sp.dma_start(w2[:, :], a["l1_w2"]).then_inc(w3_in, 16)
                    sp.dma_start(rows3[:, :], a["bias_rows"].to_broadcast([P, NROW])).then_inc(w3_in, 16)

                @block.gpsimd
                def _(pool):
                    for t in range(NT):
                        n = rows(t)
                        after(pool, step, TS * (t - RING + 1))
                        for b in range(2):
                            pool.indirect_dma_start(
                                back[0:n, t % RING, b, :], None, expert_out[b],
                                bass.IndirectOffsetOnAxis(ap=slot[0:n, 2 * t + b:2 * t + b + 1], axis=0)).then_inc(got[t], 16)

                @block.tensor
                def _(pe):
                    def strip(t):
                        for i, (first, last) in enumerate(((0, 4), (4, 8), (8, NT))):
                            if i < 2:
                                after(pe, act_saved, 2 * (t - 1) + i + 1)
                            else:
                                after(pe, saved, t)
                            for s in range(first, last):
                                m = pe.transpose(PS[i][:, (s - first) * P:(s - first + 1) * P], A[:, s, t * P:(t + 1) * P], ident[:, :])
                            m.then_inc(turned, 1)

                    def turn_x(t):
                        pe.wait_ge(normed, t + 1)
                        after(pe, x_saved, t)
                        for k in range(KD):
                            m = pe.transpose(X_PS[:, k * P:(k + 1) * P], staged[:, t % 2, k * P:(k + 1) * P], ident[:, :])
                        m.then_inc(x_turned, 1)

                    def first_product(t):
                        pe.wait_ge(x_saved, t + 1)
                        after(pe, mt_saved, 2 * t)
                        for f in range(2):
                            for k in range(KD):
                                m = pe.matmul(MT_PS[:, f * P:(f + 1) * P], wm[:, k, f * P:(f + 1) * P], turned_x[:, t % 2, k, :],
                                              start=(k == 0), stop=(k == KD - 1))
                        m.then_inc(mt_mm, 1)

                    def second_product(t):
                        pe.wait_ge(mt_saved, 2 * t + 2)
                        after(pe, m_saved, 2 * t)
                        for f in range(2):
                            m = pe.matmul(M_PS[:, 0:2 * P], MT[:, t % 2, f, :], w1[:, f:KD:2, :], start=(f == 0), stop=(f == 1))
                        m.then_inc(m_mm, 1)

                    pe.wait_ge(bias2_in, 16)
                    for t in range(NT + 3):
                        if t < NT:
                            after(pe, step, TS * (t - 1) + 1)
                            pe.matmul(BIAS_PS[:, :], gated_hot[0:2 * NE + 1, t * P:(t + 1) * P], bias2[:, :],
                                      start=True, stop=True).then_inc(bias_mm, 1)
                            strip(t)
                        if t == 2:
                            pe.wait_ge(w3_in, 64)
                        if 0 <= t - 3:
                            second_product(t - 3)
                        if 0 <= t - 2 < NT:
                            first_product(t - 2)
                        if 0 <= t - 1 < NT:
                            turn_x(t - 1)
                        if t == NT:
                            pe.wait_ge(saved, NT)
                            pe.wait_ge(act_saved, 2 * NT)
                            for s in range(NT):
                                pe.wait_ge(diags, s + 1)
                                pe.matmul(INV_PS[s // 4][:, (s % 4) * P:(s % 4 + 1) * P], ones[:, :], diag[:, s % 2, :],
                                          start=True, stop=True).then_inc(rows_mm, 1)

                @block.scalar
                def _(act):
                    for t in range(NT + 3):
                        if 0 <= t - 1 < NT:
                            act.wait_ge(aggr, t)
                            act.activation(std[:, t - 1:t], mv[:, t - 1, 1:2], ACT.Sqrt, bias=eps[:, 0:1]).then_inc(root, 1)
                        if t < NT:
                            act.activation(unused[:, :], A[:, t, 0:NP], ACT.Copy, accum_out=total[:, t:t + 1]).then_inc(sums, 1)
                            for i in range(2):
                                act.wait_ge(turned, 3 * t + i + 1)
                                act.copy(AT[:, t, 4 * i * P:4 * (i + 1) * P], PS[i][:, :]).then_inc(act_saved, 1)
                            act.wait_ge(sums, t + 1)
                        if 0 <= t - 3:
                            s = t - 3
                            act.wait_ge(m_mm, s + 1)
                            act.copy(M[0][:, s, :], M_PS[:, 0:P]).then_inc(m_saved, 1)
                            act.wait_ge(inv_step, 2 * s + 2)
                            act.activation(M[1][:, s, :], M_PS[:, P:2 * P], ACT.Copy, scale=inv[:, s:s + 1]).then_inc(m_saved, 1)
                        if 0 <= t - 2 < NT:
                            s = t - 2
                            act.wait_ge(mt_mm, s + 1)
                            after(act, m_mm, s - 1)
                            for f in range(2):
                                col = BIAS_COLS["bm"] + f
                                act.activation(MT[:, s % 2, f, :], MT_PS[:, f * P:(f + 1) * P], ACT.Identity,
                                               bias=bcol[:, col:col + 1]).then_inc(mt_saved, 1)
                        if 0 <= t - 1 < NT:
                            s = t - 1
                            act.wait_ge(x_turned, s + 1)
                            after(act, mt_mm, s - 1)
                            act.copy(turned_x[:, s % 2, :, :], X_PS[:, :].rearrange("p (k n) -> p k n", k=KD)).then_inc(x_saved, 1)
                    for i in range(0, NT, 4):
                        n = min(4, NT - i)
                        act.wait_ge(rows_mm, i + n)
                        act.copy(inv_all[:, i * P:(i + n) * P], INV_PS[i // 4][:, 0:n * P]).then_inc(rows_saved, 1)

                @block.vector
                def _(dve):
                    ch = Chain(dve, step)

                    def norm(t):
                        dve.wait_ge(root, t + 1)
                        dve.reciprocal(rstd[:, t:t + 1], std[:, t:t + 1]).then_inc(rstd_done, 1)
                        dve.wait_ge(rstd_done, t + 1)
                        after(dve, x_turned, t - 1)
                        dve.tensor_scalar(staged[:, t % 2, :], X[:, t, :], mv[:, t, 0:1], rstd[:, t:t + 1],
                                          ALU.subtract, ALU.mult).then_inc(normed, 1)

                    for t in range(NT):
                        n = rows(t)
                        dve.wait_ge(bias_mm, t + 1)
                        ch.mark(dve.tensor_tensor(X[:, t, :], X[:, t, :], BIAS_PS[:, :], ALU.add))
                        dve.wait_ge(turned, 3 * t + 3)
                        dve.tensor_copy(AT[:, t, 8 * P:NP], PS[2][:, 0:2 * P]).then_inc(saved, 1)
                        dve.wait_ge(sums, t + 1)
                        dve.tensor_scalar(inv[:, t:t + 1], total[:, t:t + 1], 1e-6, None, ALU.add).then_inc(inv_step, 1)
                        dve.tensor_scalar(valid[:, t:t + 1], total[:, t:t + 1], 0.0, None, ALU.is_gt).then_inc(valid_done, 1)
                        if t:
                            norm(t - 1)
                        dve.wait_ge(inv_step, 2 * t + 1)
                        dve.reciprocal(inv[:, t:t + 1], inv[:, t:t + 1]).then_inc(inv_step, 1)
                        dve.wait_ge(got[t], 32)
                        for b in range(2):
                            ch.wait()
                            ch.mark(dve.scalar_tensor_tensor(out=X[0:n, t, :], in0=back[0:n, t % RING, b, :],
                                                             scalar=gate[0:n, 2 * t + b:2 * t + b + 1], in1=X[0:n, t, :],
                                                             op0=ALU.mult, op1=ALU.add))
                        ch.wait()
                        ch.mark(dve.bn_stats(stats[:, t, :], X[:, t, :]))
                        assert ch.n == TS * (t + 1)
                        ch.wait()
                        dve.bn_aggr(mv[:, t, :], stats[:, t, :]).then_inc(aggr, 1)
                    norm(NT - 1)
                    dve.wait_ge(inv_step, 2 * NT)
                    for t in range(NT):
                        after(dve, rows_mm, t - 1)
                        dve.tensor_scalar(diag[:, t % 2, :], ident[:, :], inv[:, t:t + 1], None, ALU.mult).then_inc(diags, 1)
            wt = [sb(g3, f"mix_w{i}", [P, KD, D]) for i in range(2)]
            rows4 = bias_row("ffn_b2")
            w4_in, masked = sems(g3, "mix_w_in", "masked")

            with ExitStack() as ctx:
                out_part = sb(ctx, "out_part", [P, CH])
                h1 = sb(ctx, "h1", [P, CH])
                hn = sb(ctx, "hn", [P, TPC, P])
                hnT = sb(ctx, "hnT", [P, CH])
                y3 = sb(ctx, "y3", [P, TPC, D])
                st3 = sb(ctx, "st3", [P, TPC, 6])
                mv3 = sb(ctx, "mv3", [P, TPC, 2])
                idle = sb(ctx, "idle", [P, 1])
                sd3 = sb(ctx, "sd3", [P, TPC])
                XT = AT[:, 0:KD, :]
                H = sb(ctx, "H4", [P, KD, CH])
                st4 = sb(ctx, "st4", [P, TPC, 6])
                mv4 = sb(ctx, "mv4", [P, TPC, 2])
                std4 = sb(ctx, "std4", [P, TPC])
                rstd4 = sb(ctx, "rstd4", [P, TPC])
                aggr, root, rstd_done, normed, x_turned, x_saved = sems(
                    ctx, "aggr4", "root4", "rstd4", "normed4", "x_turned4", "x_saved4")
                up_mm, h_saved, down_mm, out_added, x_out = sems(ctx, "mix_up_mm", "mix_h", "mix_down_mm", "mix_added", "x_out")
                out_mm_, in_mm, part_saved, h1_saved, h1_T, stat3, root3, hn_ready, hn_T, hnT_saved, out_mm, out_step, x_stats = sems(
                    ctx, "outgoing_mm", "incoming_mm", "part_saved", "h1_saved", "h1_T", "stat3", "root3", "hn_ready", "hn_T",
                    "hnT_saved", "out_mm3", "out_step3", "x_stats3")
                block = ctx.enter_context(nc.Block())

                @block.sync
                def _(sp):
                    for i in range(2):
                        sp.dma_start(wt[i][:, :, :], a[f"mix_w{i + 1}"].rearrange("(k p) s -> p k s", p=P)).then_inc(w4_in, 16)
                    last = TPC * (NC - 1)
                    with sp.Fori(0, NC - 1) as c:
                        sp.wait_ge(out_added, 2 * TPC * c + 2 * TPC)
                        sp.dma_start(out[ds(c * CH, CH), :].rearrange("(t p) d -> p t d", p=P), X[:, ds(TPC * c, TPC), :]).then_inc(x_out, 16)
                    sp.wait_ge(out_added, 2 * NT)
                    sp.dma_start(out[last * P:(NT - 1) * P, :], X[:, last, :]).then_inc(x_out, 16)
                    sp.dma_start(out[(NT - 1) * P:N, :], X[0:LAST, NT - 1, :]).then_inc(x_out, 16)
                    sp.wait_ge(x_out, 16 * (NC + 1))

                @block.gpsimd
                def _(pool):
                    pool.wait_ge(w4_in, 32)
                    for i in range(2):
                        for k in range(KD):
                            w = wt[i][:, k, k * P:(k + 1) * P]
                            pool.affine_select(out=w, in_=w, compare_op=ALU.is_ge, fill=0.0, base=0, pattern=[[1, P]],
                                               channel_multiplier=-1).then_inc(masked, 1)
                LNS, OUTS = 11, 6

                def outgoing(pe, c, first, last):
                    if first == 0:
                        after(pe, part_saved, c)
                    for s in range(first, last):
                        m = pe.matmul(PS[0][:, 0:CH], M[0][:, s, :], AT[:, s, ds(c * CH, CH)], start=(s == 0), stop=(s == NT - 1))
                    if last == NT:
                        m.then_inc(out_mm_, 1)

                def incoming(pe, c, first, last):
                    if first == 0:
                        after(pe, h1_saved, c)
                    for s in range(first, last):
                        m = pe.matmul(PS[1][:, 0:CH], M[1][:, s, :], A[:, s, ds(c * CH, CH)], start=(s == 0), stop=(s == NT - 1))
                    if last == NT:
                        m.then_inc(in_mm, 1)

                def turn_h1(pe, c):
                    pe.wait_ge(h1_saved, c + 1)
                    after(pe, hn_ready, c)
                    for j in range(TPC):
                        m = pe.transpose(PS[3][:, j * P:(j + 1) * P], h1[:, j * P:(j + 1) * P], ident[:, :])
                    m.then_inc(h1_T, 1)

                def turn_hn(pe, c):
                    pe.wait_ge(hn_ready, c + 1)
                    after(pe, hnT_saved, c)
                    for j in range(TPC):
                        m = pe.transpose(PS[4][:, j * P:(j + 1) * P], hn[:, j, :], ident[:, :])
                    m.then_inc(hn_T, 1)

                def dense2(pe, c):
                    pe.wait_ge(hnT_saved, c + 1)
                    after(pe, out_step, OUTS * c)
                    for j in range(TPC):
                        m = pe.matmul(PS[5 + j][:, :], hnT[:, j * P:(j + 1) * P], w2[:, :], start=True, stop=True)
                    m.then_inc(out_mm, 1)

                def turn_x(pe, c):
                    pe.wait_ge(normed, TPC * c + TPC)
                    after(pe, x_saved, TPC * c)
                    for j in range(TPC):
                        for k in range(KD):
                            m = pe.transpose(PS[(2, 7)[j]][:, k * P:(k + 1) * P], y3[:, j, k * P:(k + 1) * P], ident[:, :])
                    m.then_inc(x_turned, 1)

                def mix_up(pe, c):
                    pe.wait_ge(x_saved, TPC * c + TPC)
                    for s in range(KD):
                        after(pe, h_saved, KD * c + s - 1)
                        for k in range(s + 1):
                            m = pe.matmul(PS[s % 2][:, 0:CH], wt[0][:, k, s * P:(s + 1) * P], XT[:, k, ds(c * CH, CH)],
                                          start=(k == 0), stop=(k == s))
                        m.then_inc(up_mm, 1)

                def mix_down(pe, c):
                    pe.wait_ge(h_saved, KD * c + KD)
                    for j in range(TPC):
                        after(pe, out_added, 2 * TPC * c)
                        for k in range(KD):
                            m = pe.matmul(PS[3 + j][:, k * P:D], H[:, k, j * P:(j + 1) * P], wt[1][:, k, k * P:D],
                                          start=(k == 0), stop=(k == KD - 1), skip_group_check=True)
                        m.then_inc(down_mm, 1)

                @block.tensor
                def _(pe):
                    outgoing(pe, 0, 0, NT)
                    incoming(pe, 0, 0, NT)

                    def chunk(c, before, x_before):
                        outgoing(pe, c, 0, 3)
                        turn_h1(pe, before)
                        outgoing(pe, c, 3, NT)
                        incoming(pe, c, 0, 6)
                        turn_hn(pe, before)
                        incoming(pe, c, 6, 9)
                        dense2(pe, before)
                        if x_before is not None:
                            turn_x(pe, x_before)
                        incoming(pe, c, 9, NT)
                    chunk(1, 0, None)
                    with pe.Fori(2, NC) as c:
                        chunk(c, c - 1, c - 2)
                    turn_h1(pe, NC - 1)
                    pe.wait_ge(masked, 2 * KD)
                    mix_up(pe, 0)
                    turn_hn(pe, NC - 1)
                    pe.wait_ge(hnT_saved, NC)
                    mix_down(pe, 0)
                    turn_x(pe, NC - 2)
                    dense2(pe, NC - 1)
                    mix_up(pe, 1)
                    mix_down(pe, 1)
                    turn_x(pe, NC - 1)
                    with pe.Fori(2, NC) as c:
                        mix_up(pe, c)
                        mix_down(pe, c)

                @block.scalar
                def _(act):
                    def root_h(c):
                        act.wait_ge(stat3, LNS * c + 2 * TPC)
                        act.activation(sd3[:, :], mv3[:, :, 1], ACT.Sqrt, bias=eps[:, 0:1]).then_inc(root3, 1)

                    def save_hn(c):
                        act.wait_ge(hn_T, c + 1)
                        after(act, out_mm, c)
                        act.copy(hnT[:, :], PS[4][:, 0:CH]).then_inc(hnT_saved, 1)

                    def root_x(c):
                        act.wait_ge(aggr, TPC * c + TPC)
                        act.activation(std4[:, :], mv4[:, :, 1], ACT.Sqrt, bias=eps[:, 0:1]).then_inc(root, 1)

                    def save_x(c):
                        act.wait_ge(x_turned, c + 1)
                        for j in range(TPC):
                            act.copy(XT[:, :, ds(c * CH + j * P, P)], PS[(2, 7)[j]][:, :].rearrange("p (k n) -> p k n", k=KD)).then_inc(x_saved, 1)

                    def gelu(c):
                        for s in range(KD):
                            act.wait_ge(up_mm, KD * c + s + 1)
                            after(act, down_mm, TPC * c)
                            col = BIAS_COLS["ffn_b1"] + s
                            act.activation(H[:, s, :], PS[s % 2][:, 0:CH], ACT.Gelu, bias=bcol[:, col:col + 1]).then_inc(h_saved, 1)

                    root_h(0)
                    save_hn(0)
                    with act.Fori(1, NC - 1) as c:
                        root_h(c)
                        root_x(c - 1)
                        save_hn(c)
                        save_x(c - 1)
                    root_h(NC - 1)
                    root_x(NC - 2)
                    gelu(0)
                    save_hn(NC - 1)
                    save_x(NC - 2)
                    gelu(1)
                    root_x(NC - 1)
                    save_x(NC - 1)
                    with act.Fori(2, NC) as c:
                        gelu(c)

                @block.vector
                def _(dve):
                    def outgoing_part(c):
                        dve.wait_ge(out_mm_, c + 1)
                        dve.tensor_tensor(out_part[:, :], PS[0][:, 0:CH], inv_all[:, ds(c * CH, CH)], ALU.mult).then_inc(part_saved, 1)

                    def sum_parts(c):
                        dve.wait_ge(part_saved, c + 1)
                        dve.wait_ge(in_mm, c + 1)
                        after(dve, h1_T, c)
                        dve.scalar_tensor_tensor(out=h1[:, :], in0=PS[1][:, 0:CH],
                                                 scalar=bcol[:, BIAS_COLS["l1_b1"]:BIAS_COLS["l1_b1"] + 1], in1=out_part[:, :],
                                                 op0=ALU.add, op1=ALU.add).then_inc(h1_saved, 1)

                    def norm(c):
                        ch = Chain(dve, stat3)
                        ch.at(LNS * c)
                        dve.wait_ge(h1_T, c + 1)
                        after(dve, hn_T, c)
                        for j in range(TPC):
                            ch.mark(dve.bn_stats(st3[:, j, :], PS[3][:, j * P:(j + 1) * P]))
                        ch.wait()
                        dve.memset(idle[:, :], 0.0)
                        ch.mark(dve.bn_aggr(mv3[:, 0, :], st3[:, 0, :]))
                        ch.mark(dve.bn_aggr(mv3[:, 1, :], st3[:, 1, :]))
                        dve.wait_ge(root3, c + 1)
                        ch.mark(dve.reciprocal(sd3[:, :], sd3[:, :]))
                        ch.wait()
                        for j in range(TPC):
                            ch.mark(dve.tensor_scalar(hn[:, j, :], PS[3][:, j * P:(j + 1) * P], mv3[:, j, 0:1], sd3[:, j:j + 1],
                                                      ALU.subtract, ALU.mult))
                        ch.wait()
                        for j in range(TPC):
                            ch.mark(dve.tensor_tensor(hn[:, j, :], hn[:, j, :], bias_row("gamma"), ALU.mult))
                        ch.wait()
                        for j in range(TPC):
                            ch.mark(dve.tensor_tensor(hn[:, j, :], hn[:, j, :], bias_row("beta"), ALU.add))
                        ch.wait()
                        assert ch.n == LNS
                        dve.tensor_scalar(hn[:, :, :], hn[:, :, :], 0.0, None, ALU.max).then_inc(hn_ready, 1)

                    def add(c):
                        ch = Chain(dve, out_step)
                        ch.at(OUTS * c)
                        dve.wait_ge(out_mm, c + 1)
                        after(dve, x_turned, c)
                        for j in range(TPC):
                            ch.mark(dve.tensor_tensor(y3[:, j, :], PS[5 + j][:, :], bias_row("l1_b2"), ALU.add))
                        ch.wait()
                        for j in range(TPC):
                            ch.mark(dve.tensor_scalar(y3[:, j, :], y3[:, j, :], 0.0, valid[:, ds(TPC * c + j, 1)], ALU.max, ALU.mult))
                        ch.wait()
                        for j in range(TPC):
                            x_t = tile_of(X, TPC * c + j)
                            ch.mark(dve.tensor_tensor(x_t, x_t, y3[:, j, :], ALU.add))
                        assert ch.n == OUTS
                    def norm_x(c):
                        dve.wait_ge(out_step, OUTS * c + OUTS)
                        dve.memset(idle[:, :], 0.0)
                        for j in range(TPC):
                            dve.bn_stats(st4[:, j, :], tile_of(X, TPC * c + j)).then_inc(x_stats, 1)
                        dve.wait_ge(x_stats, TPC * c + TPC)
                        dve.memset(idle[:, :], 0.0)
                        for j in range(TPC):
                            dve.bn_aggr(mv4[:, j, :], st4[:, j, :]).then_inc(aggr, 1)
                        dve.wait_ge(root, c + 1)
                        dve.reciprocal(rstd4[:, :], std4[:, :]).then_inc(rstd_done, 1)
                        dve.wait_ge(rstd_done, c + 1)
                        for j in range(TPC):
                            t = TPC * c + j
                            dve.tensor_scalar(y3[:, j, :], tile_of(X, t), mv4[:, j, 0:1], rstd4[:, j:j + 1],
                                              ALU.subtract, ALU.mult).then_inc(normed, 1)

                    def mix_add(c):
                        for j in range(TPC):
                            x_t = tile_of(X, TPC * c + j)
                            dve.wait_ge(down_mm, TPC * c + j + 1)
                            dve.tensor_tensor(x_t, x_t, PS[3 + j][:, :], ALU.add).then_inc(out_added, 1)
                            dve.wait_ge(out_added, 2 * TPC * c + 2 * j + 1)
                            dve.tensor_tensor(x_t, x_t, rows4, ALU.add).then_inc(out_added, 1)
                    outgoing_part(0)
                    sum_parts(0)

                    def chunk(c, before, x_before):
                        norm(before)
                        outgoing_part(c)
                        if x_before is not None:
                            norm_x(x_before)
                        sum_parts(c)
                        add(before)
                    chunk(1, 0, None)
                    with dve.Fori(2, NC) as c:
                        chunk(c, c - 1, c - 2)
                    norm(NC - 1)
                    norm_x(NC - 2)
                    mix_add(0)
                    add(NC - 1)
                    norm_x(NC - 1)
                    mix_add(1)
                    with dve.Fori(2, NC) as c:
                        mix_add(c)


_COLS = [("gnn_b1", "L0_gnn_b1"), ("gnn_br1", "L0_gnn_br1"), ("gnn_b2", "L0_gnn_b2"), ("gnn_br2", "L0_gnn_br2"),
         ("bs1", "L0_ffn_bs1"), ("l1_b1", "L1_gnn_b1"), ("ffn_b1", "L1_ffn_b1"), ("bm", "L1_gnn_bm")]
_ROWS = [("gamma", "L1_gnn_gamma"), ("beta", "L1_gnn_beta"),
         ("l1_b2", "L1_gnn_b2"), ("ffn_b2", "L1_ffn_b2")]


def _laid_out(inputs):
    import numpy as np
    g = {k: np.asarray(v) for k, v in inputs.items()}
    a = {k: g[k] for k in ("x", "src", "dst", "edge_weight")}
    a["bias_cols"] = np.ascontiguousarray(np.concatenate([g[n].reshape(-1, P).T for _, n in _COLS], axis=1))
    a["bias_rows"] = np.concatenate([g[n] for _, n in _ROWS]).reshape(1, -1)
    for l in "12":
        a["gnn_w" + l] = np.ascontiguousarray(g["L0_gnn_W" + l].T)
        a["gate_w" + l] = np.ascontiguousarray(g["L0_gnn_Wr" + l].T)
    a["router_w"] = np.ascontiguousarray(np.concatenate([g["L0_ffn_Wr_sp"], g["L0_ffn_Wr_fq"]], axis=1))
    a["router_b"] = np.concatenate([g["L0_ffn_br_sp"], g["L0_ffn_br_fq"]]).reshape(-1, 1)
    a["ws1"], a["ws2"] = g["L0_ffn_Ws1"], g["L0_ffn_Ws2"]
    for b in ("sp", "fq"):
        for n in ("W1", "b1", "W2"):
            a[f"{n}_{b}"] = g[f"L0_ffn_{n}_{b}"]
    a["b2_all"] = np.concatenate([g["L0_ffn_b2_sp"], g["L0_ffn_b2_fq"], g["L0_ffn_bs2"].reshape(1, -1)], axis=0)
    a["wm"], a["l1_w1"], a["l1_w2"] = g["L1_gnn_Wm"], g["L1_gnn_W1"], g["L1_gnn_W2"]
    a["mix_w1"] = np.ascontiguousarray(g["L1_ffn_W1"].T)
    a["mix_w2"] = np.ascontiguousarray(g["L1_ffn_W2"].T)
    return a


def _program(nc, arrays):
    aps = {k: nc.dram_tensor(f"in_{k}", v.shape, mybir.dt.from_np(v.dtype), kind="ExternalInput").ap()
           for k, v in arrays.items()}
    out = nc.dram_tensor("out_x", (N, D), F32, kind="ExternalOutput").ap()
    routed = [nc.dram_tensor(f"routed{b}", (SLOTS, D), F32, kind="Internal").ap() for b in range(2)]
    expert_out = [nc.dram_tensor(f"expert_out{b}", (SLOTS, D), F32, kind="Internal").ap() for b in range(2)]
    build(nc, aps, out, routed, expert_out)


def kernel(**inputs):
    import concourse.bacc as bacc
    from concourse.bass_utils import run_bass_kernel_spmd
    arrays = _laid_out(inputs)
    nc = bacc.Bacc("TRN2", target_bir_lowering=False, num_devices=1)
    _program(nc, arrays)
    r = run_bass_kernel_spmd(nc, [{f"in_{k}": v for k, v in arrays.items()}], core_ids=[0])
    return r.results[0]["out_x"]
```
